# Optimizing a Trainium2 kernel written in Bass

```python
import numpy as np
import jax
import jax.numpy as jnp

def _softmax(x, axis=-1):
    return jax.nn.softmax(x, axis=axis)

def _gelu(x):
    return jax.nn.gelu(x, approximate=True)

def _silu(x):
    return jax.nn.silu(x)

def _sigmoid(x):
    return jax.nn.sigmoid(x)

def _layernorm(x, axis=-1, eps=1e-05):
    m = jnp.mean(x, axis=axis, keepdims=True)
    v = jnp.var(x, axis=axis, keepdims=True)
    return (x - m) / jnp.sqrt(v + eps)

def _scatter_add(tgt, idx, src, axis=0):
    return tgt.at[idx].add(src)

def _segment_sum(src, seg, n):
    return jax.ops.segment_sum(src, seg, n)
kernel_name = 'mk_conv_preact_d2_conv_nhwc768_r4_8ce5f4'

def setup_inputs(seed: int=0):
    np.random.seed(seed)
    _w = jnp.asarray

    def _rec_inputs():
        import jax
        import jax.numpy as jnp
        _gk = jax.random.key(seed)
        x = -0.0005963 + 1.001 * jax.random.normal(jax.random.fold_in(_gk, 1), (1, 16, 16, 192), jnp.float32)
        return x
    x = _rec_inputs()

    def _L0_conv_setup():
        import jax, jax.numpy as jnp
        import numpy as np
        NUM_HEADS = 12
        HEAD_DIM = 16
        DIM = NUM_HEADS * HEAD_DIM
        EPS = 1e-05

        def layer_norm(x, g, b):
            m = jnp.mean(x, axis=-1, keepdims=True)
            v = jnp.mean(jnp.square(x - m), axis=-1, keepdims=True)
            return (x - m) * jax.lax.rsqrt(v + EPS) * g + b

        def dwconv3x3(x, w):
            return jax.lax.conv_general_dilated(x, w, window_strides=(1, 1), padding=[(1, 1), (1, 1)], dimension_numbers=('NHWC', 'HWIO', 'NHWC'), feature_group_count=x.shape[-1])
        key = jax.random.key(seed)
        ks = jax.random.split(key, 16)
        d = {}
        d['x'] = jax.random.normal(ks[0], (1, 16, 16, DIM), jnp.float32)
        d['w_qkv'] = jax.random.normal(ks[1], (3 * DIM, DIM), jnp.float32) * 0.02
        d['b_qkv'] = jnp.zeros((3 * DIM,), jnp.float32)
        d['w_pool_q'] = jax.random.normal(ks[2], (3, 3, 1, HEAD_DIM), jnp.float32) * 0.1
        d['w_pool_k'] = jax.random.normal(ks[3], (3, 3, 1, HEAD_DIM), jnp.float32) * 0.1
        d['w_pool_v'] = jax.random.normal(ks[4], (3, 3, 1, HEAD_DIM), jnp.float32) * 0.1
        d['g_q'] = jnp.ones((HEAD_DIM,), jnp.float32)
        d['b_q'] = jnp.zeros((HEAD_DIM,), jnp.float32)
        d['g_k'] = jnp.ones((HEAD_DIM,), jnp.float32)
        d['b_k'] = jnp.zeros((HEAD_DIM,), jnp.float32)
        d['g_v'] = jnp.ones((HEAD_DIM,), jnp.float32)
        d['b_v'] = jnp.zeros((HEAD_DIM,), jnp.float32)
        d['rel_pos_h'] = jax.random.normal(ks[5], (127, HEAD_DIM), jnp.float32) * 0.02
        d['rel_pos_w'] = jax.random.normal(ks[6], (127, HEAD_DIM), jnp.float32) * 0.02
        d['w_proj'] = jax.random.normal(ks[7], (DIM, DIM), jnp.float32) * 0.02
        d['b_proj'] = jnp.zeros((DIM,), jnp.float32)
        return d
    _L0_conv_all = _L0_conv_setup()
    _L0_conv_in = {k: v for k, v in _L0_conv_all.items() if k in ('w_qkv', 'b_qkv', 'w_pool_q', 'w_pool_k', 'w_pool_v', 'g_q', 'b_q', 'g_k', 'b_k', 'g_v', 'b_v', 'rel_pos_h', 'rel_pos_w', 'w_proj', 'b_proj')}
    del _L0_conv_all

    def _L1_conv_setup():
        import jax, jax.numpy as jnp
        import numpy as np
        NUM_HEADS = 12
        FACT_S = 1.0
        DIM = 192
        RANK = 16
        HGRID = 48

        def get_rel_pos(q_size, k_size, rel_pos):
            q_coords = jnp.arange(q_size)[:, None] * max(k_size / q_size, 1.0)
            k_coords = jnp.arange(k_size)[None, :] * max(q_size / k_size, 1.0)
            rel = (q_coords - k_coords + (k_size - 1) * max(q_size / k_size, 1.0)).astype(jnp.int32)
            return rel_pos[rel]
        key = jax.random.key(seed)
        ks = jax.random.split(key, 10)
        w = 1.0 / np.sqrt(DIM)
        return {'x': jax.random.normal(ks[0], (1, HGRID, HGRID, DIM), jnp.float32), 'qkv_w': jax.random.normal(ks[1], (DIM, 3 * DIM), jnp.float32) * w, 'qkv_b': jnp.zeros((3 * DIM,), jnp.float32), 'FacTu_w': jax.random.normal(ks[2], (DIM, RANK), jnp.float32) * w, 'q_facts_w': jax.random.normal(ks[3], (RANK, RANK), jnp.float32) * 0.25, 'v_facts_w': jax.random.normal(ks[4], (RANK, RANK), jnp.float32) * 0.25, 'FacTv_w': jax.random.normal(ks[5], (RANK, DIM), jnp.float32) * 0.25, 'rel_pos_h': jax.random.normal(ks[6], (2 * HGRID - 1, DIM // NUM_HEADS), jnp.float32) * 0.02, 'rel_pos_w': jax.random.normal(ks[7], (2 * HGRID - 1, DIM // NUM_HEADS), jnp.float32) * 0.02, 'proj_w': jax.random.normal(ks[8], (DIM, DIM), jnp.float32) * w, 'proj_b': jnp.zeros((DIM,), jnp.float32)}
    _L1_conv_all = _L1_conv_setup()
    _L1_conv_in = {k: v for k, v in _L1_conv_all.items() if k in ('qkv_w', 'qkv_b', 'FacTu_w', 'q_facts_w', 'v_facts_w', 'FacTv_w', 'rel_pos_h', 'rel_pos_w', 'proj_w', 'proj_b')}
    del _L1_conv_all
    return {'x': x, 'L0_conv_w_qkv': _L0_conv_in['w_qkv'], 'L0_conv_b_qkv': _L0_conv_in['b_qkv'], 'L0_conv_w_pool_q': _L0_conv_in['w_pool_q'], 'L0_conv_w_pool_k': _L0_conv_in['w_pool_k'], 'L0_conv_w_pool_v': _L0_conv_in['w_pool_v'], 'L0_conv_g_q': _L0_conv_in['g_q'], 'L0_conv_b_q': _L0_conv_in['b_q'], 'L0_conv_g_k': _L0_conv_in['g_k'], 'L0_conv_b_k': _L0_conv_in['b_k'], 'L0_conv_g_v': _L0_conv_in['g_v'], 'L0_conv_b_v': _L0_conv_in['b_v'], 'L0_conv_rel_pos_h': _L0_conv_in['rel_pos_h'], 'L0_conv_rel_pos_w': _L0_conv_in['rel_pos_w'], 'L0_conv_w_proj': _L0_conv_in['w_proj'], 'L0_conv_b_proj': _L0_conv_in['b_proj'], 'L1_conv_qkv_w': _L1_conv_in['qkv_w'], 'L1_conv_qkv_b': _L1_conv_in['qkv_b'], 'L1_conv_FacTu_w': _L1_conv_in['FacTu_w'], 'L1_conv_q_facts_w': _L1_conv_in['q_facts_w'], 'L1_conv_v_facts_w': _L1_conv_in['v_facts_w'], 'L1_conv_FacTv_w': _L1_conv_in['FacTv_w'], 'L1_conv_rel_pos_h': _L1_conv_in['rel_pos_h'], 'L1_conv_rel_pos_w': _L1_conv_in['rel_pos_w'], 'L1_conv_proj_w': _L1_conv_in['proj_w'], 'L1_conv_proj_b': _L1_conv_in['proj_b']}

def reference(x, L0_conv_w_qkv, L0_conv_b_qkv, L0_conv_w_pool_q, L0_conv_w_pool_k, L0_conv_w_pool_v, L0_conv_g_q, L0_conv_b_q, L0_conv_g_k, L0_conv_b_k, L0_conv_g_v, L0_conv_b_v, L0_conv_rel_pos_h, L0_conv_rel_pos_w, L0_conv_w_proj, L0_conv_b_proj, L1_conv_qkv_w, L1_conv_qkv_b, L1_conv_FacTu_w, L1_conv_q_facts_w, L1_conv_v_facts_w, L1_conv_FacTv_w, L1_conv_rel_pos_h, L1_conv_rel_pos_w, L1_conv_proj_w, L1_conv_proj_b):
    import jax
    import jax.numpy as jnp

    def _L0_conv_ref(x, w_qkv, b_qkv, w_pool_q, w_pool_k, w_pool_v, g_q, b_q, g_k, b_k, g_v, b_v, rel_pos_h, rel_pos_w, w_proj, b_proj):
        import jax, jax.numpy as jnp
        import numpy as np
        NUM_HEADS = 12
        HEAD_DIM = 16
        DIM = NUM_HEADS * HEAD_DIM
        EPS = 1e-05

        def layer_norm(x, g, b):
            m = jnp.mean(x, axis=-1, keepdims=True)
            v = jnp.mean(jnp.square(x - m), axis=-1, keepdims=True)
            return (x - m) * jax.lax.rsqrt(v + EPS) * g + b

        def dwconv3x3(x, w):
            return jax.lax.conv_general_dilated(x, w, window_strides=(1, 1), padding=[(1, 1), (1, 1)], dimension_numbers=('NHWC', 'HWIO', 'NHWC'), feature_group_count=x.shape[-1])
        B, H, W, _ = x.shape
        nh, hd = (NUM_HEADS, HEAD_DIM)
        scale = hd ** (-0.5)
        qkv = x @ w_qkv.T + b_qkv
        qkv = qkv.reshape(B, H, W, 3, nh, hd).transpose(3, 0, 4, 1, 2, 5)
        qkv = qkv.reshape(3, B * nh, H, W, hd)
        q, k, v = (qkv[0], qkv[1], qkv[2])
        q = layer_norm(dwconv3x3(q, w_pool_q), g_q, b_q)
        k = layer_norm(dwconv3x3(k, w_pool_k), g_k, b_k)
        v = layer_norm(dwconv3x3(v, w_pool_v), g_v, b_v)
        ori_q = q
        qf = q.reshape(B * nh, H * W, hd)
        kf = k.reshape(B * nh, H * W, hd)
        vf = v.reshape(B * nh, H * W, hd)
        attn = jnp.einsum('bqc,bkc->bqk', qf * scale, kf)
        coords = jnp.arange(H)
        rel_idx = coords[:, None] - coords[None, :] + (H - 1)
        Rh = rel_pos_h[rel_idx]
        Rw = rel_pos_w[rel_idx]
        r_q = qf.reshape(B * nh, H, W, hd)
        rel_h = jnp.einsum('bhwc,hkc->bhwk', r_q, Rh)
        rel_w = jnp.einsum('bhwc,wkc->bhwk', r_q, Rw)
        attn = attn.reshape(B * nh, H, W, H, W) + rel_h[:, :, :, :, None] + rel_w[:, :, :, None, :]
        attn = jax.nn.softmax(attn.reshape(B * nh, H * W, H * W), axis=-1)
        o = attn @ vf
        o = o.reshape(B * nh, H, W, hd) + ori_q
        o = o.reshape(B, nh, H, W, hd).transpose(0, 2, 3, 1, 4).reshape(B, H, W, nh * hd)
        return o @ w_proj.T + b_proj

    def _L1_conv_ref(x, qkv_w, qkv_b, FacTu_w, q_facts_w, v_facts_w, FacTv_w, rel_pos_h, rel_pos_w, proj_w, proj_b):
        import jax, jax.numpy as jnp
        import numpy as np
        NUM_HEADS = 12
        FACT_S = 1.0
        DIM = 192
        RANK = 16
        HGRID = 48

        def get_rel_pos(q_size, k_size, rel_pos):
            q_coords = jnp.arange(q_size)[:, None] * max(k_size / q_size, 1.0)
            k_coords = jnp.arange(k_size)[None, :] * max(q_size / k_size, 1.0)
            rel = (q_coords - k_coords + (k_size - 1) * max(q_size / k_size, 1.0)).astype(jnp.int32)
            return rel_pos[rel]
        B, H, W, C = x.shape
        nH = NUM_HEADS
        hd = C // nH
        scale = hd ** (-0.5)
        qkv = x @ qkv_w + qkv_b
        u = x @ FacTu_w
        new_q = u @ q_facts_w @ FacTv_w * FACT_S
        new_v = u @ v_facts_w @ FacTv_w * FACT_S
        qkv = qkv.at[..., :C].add(new_q).at[..., 2 * C:].add(new_v)
        qkv = qkv.reshape(B, H * W, 3, nH, hd).transpose(2, 0, 3, 1, 4)
        qkv = qkv.reshape(3, B * nH, H * W, hd)
        q, k, v = (qkv[0], qkv[1], qkv[2])
        attn = jnp.einsum('bqc,bkc->bqk', q * scale, k)
        Rh = get_rel_pos(H, H, rel_pos_h)
        Rw = get_rel_pos(W, W, rel_pos_w)
        r_q = q.reshape(B * nH, H, W, hd)
        rel_h = jnp.einsum('bhwc,hkc->bhwk', r_q, Rh)
        rel_w = jnp.einsum('bhwc,wkc->bhwk', r_q, Rw)
        attn = (attn.reshape(B * nH, H, W, H, W) + rel_h[:, :, :, :, None] + rel_w[:, :, :, None, :]).reshape(B * nH, H * W, H * W)
        attn = jax.nn.softmax(attn, axis=-1)
        out = attn @ v
        out = out.reshape(B, nH, H, W, hd).transpose(0, 2, 3, 1, 4).reshape(B, H, W, C)
        return out @ proj_w + proj_b

    def _gn(v, G=32, eps=1e-05):
        B_, H_, W_, C_ = v.shape
        g = v.reshape(B_, H_, W_, G, C_ // G)
        m = jnp.mean(g, axis=(1, 2, 4), keepdims=True)
        s = jnp.var(g, axis=(1, 2, 4), keepdims=True)
        return ((g - m) / jnp.sqrt(s + eps)).reshape(v.shape)

    def _ln_c(v, eps=1e-06):
        m = jnp.mean(v, axis=-1, keepdims=True)
        s = jnp.var(v, axis=-1, keepdims=True)
        return (v - m) / jnp.sqrt(s + eps)

    def _ln_t(v, eps=1e-05):
        m = jnp.mean(v, axis=-1, keepdims=True)
        s = jnp.var(v, axis=-1, keepdims=True)
        return (v - m) / jnp.sqrt(s + eps)

    def _to_tokens(v):
        B_, H_, W_, C_ = v.shape
        return v.reshape(B_, H_ * W_, C_)

    def _from_tokens(t, like):
        return t.reshape(like.shape)
    x = x + _L0_conv_ref(_gn(x), L0_conv_w_qkv, L0_conv_b_qkv, L0_conv_w_pool_q, L0_conv_w_pool_k, L0_conv_w_pool_v, L0_conv_g_q, L0_conv_b_q, L0_conv_g_k, L0_conv_b_k, L0_conv_g_v, L0_conv_b_v, L0_conv_rel_pos_h, L0_conv_rel_pos_w, L0_conv_w_proj, L0_conv_b_proj)
    x = x + _L1_conv_ref(_gn(x), L1_conv_qkv_w, L1_conv_qkv_b, L1_conv_FacTu_w, L1_conv_q_facts_w, L1_conv_v_facts_w, L1_conv_FacTv_w, L1_conv_rel_pos_h, L1_conv_rel_pos_w, L1_conv_proj_w, L1_conv_proj_b)
    return x

_drawn_inputs = setup_inputs


def setup_inputs(seed=0):
    import zlib

    import numpy as np

    out = dict(_drawn_inputs(seed))
    spreads = {'L0_conv_b_qkv': (0.0, 0.1),
     'L0_conv_g_q': (1.0, 0.2),
     'L0_conv_b_q': (0.0, 0.1),
     'L0_conv_g_k': (1.0, 0.6),
     'L0_conv_b_k': (0.0, 0.8),
     'L0_conv_g_v': (1.0, 0.6),
     'L0_conv_b_v': (0.0, 0.1),
     'L0_conv_b_proj': (0.0, 0.1),
     'L1_conv_qkv_b': (0.0, 0.1),
     'L1_conv_proj_b': (0.0, 0.1)}
    factors = {'L0_conv_w_pool_k': 2.7,
     'L0_conv_rel_pos_h': 8.0,
     'L0_conv_rel_pos_w': 8.0,
     'L1_conv_rel_pos_h': 2.893,
     'L1_conv_rel_pos_w': 3.014}
    for name, (base, spread) in spreads.items():
        noise = np.random.default_rng([zlib.crc32(name.encode()), seed]).standard_normal(out[name].shape)
        drawn = base * np.exp(spread * noise) if base else spread * noise
        out[name] = jnp.asarray(drawn.astype(out[name].dtype))
    for name, factor in factors.items():
        out[name] = (out[name] * factor).astype(out[name].dtype)
    return out
```

```python
from contextlib import ExitStack

import concourse.bass as bass
from concourse import mybir

F32 = mybir.dt.float32
F32R = mybir.dt.float32r
ALU = mybir.AluOpType
ACT = mybir.ActivationFunctionType
AXX = mybir.AxisListType.X

SIDE = 16
TOK = SIDE * SIDE
DIM = 192
HEADS = 12
HD = DIM // HEADS
HALF = DIM // 2
GROUP = 6
QT = TOK // 128
HG = HEADS // 4
REL = 2 * SIDE - 1
PADDED = SIDE + 2
TAPS = 9
EPS = 1e-5
WARM0, WARM1 = 9, 8

A, B, D, C, E = range(5)
PARTS = {
    A: [(0, 0, 128)],
    B: [(0, DIM, 128)],
    D: [(0, 128, 64), (64, DIM + 128, 64)],
    C: [(0, 2 * DIM, 128)],
    E: [(0, 2 * DIM + 128, 64)],
}
ROWS = {A: 128, B: 128, D: 128, C: 128, E: 64}

ID0, CEN0, AVG0, SUM0, HOT0 = 0, 128, 256, 384, 512
NCST = HOT0 + TOK
TAP0, BQKV0, LNG0, LNB0, BQKV1, BPROJ, MASK = 0, 45, 50, 55, 60, 63, 67
GRP0 = 69
NVEC = GRP0 + HALF


def q_place(h):
    return (A, h) if h < 8 else (D, h - 8)


def k_place(h):
    return (B, h) if h < 8 else (D, h - 4)


def attention_blocks(nc, x_t, w_qkv0, w_qkv1, consts, vectors, neg_hot, rel, lora, v_bias1, w_proj, w_proj_q, out_t):
    with ExitStack() as ctx:
        def sb(name, shape, dt=F32):
            return ctx.enter_context(nc.sbuf_tensor(name, shape, dt))

        def sem(name):
            return ctx.enter_context(nc.semaphore(name))

        def sems(name):
            return [sem(f"{name}_{b}") for b in range(2)]

        xs = [sb(f"x_{i}", [HALF, 2, TOK]) for i in range(3)]
        xn = sb("xn", [HALF, 2, TOK])
        stats = sb("stats", [HALF, 2, 6])
        mom = sb("mom", [HALF, 2, 2])
        sums = sb("sums", [HALF, 2, 2])
        gmean = sb("gmean", [HALF, 2, 2])
        gvar = sb("gvar", [HALF, 2])
        glog = sb("glog", [HALF, 2])
        grstd = sb("grstd", [HALF, 2])
        w0 = sb("w0", [HALF, 2, 3 * DIM])
        w1 = sb("w1", [HALF, 2, 3 * DIM])
        cst = sb("cst", [128, NCST])
        vec = sb("vec", [128, NVEC])
        nhot = sb("nhot", [128, 4 * 128])
        nhot_r = sb("nhot_r", [128, 4, 128], F32R)
        ident_r = sb("ident_r", [128, 128], F32R)
        relt = sb("relt", [128, 4, REL])
        relt_hi = sb("relt_hi", [128, 4, REL], F32R)
        relt_s = sb("relt_s", [128, 4, REL])
        rel_w = sb("rel_w", [128, 4, SIDE, 64], F32R)
        lo_w = sb("lo_w", [16, 2 * DIM + 32])
        lo_t = sb("lo_t", [16, 2, DIM])
        vb1 = sb("vb1", [128, DIM])
        wp = sb("wp", [128, 2, HG, DIM])
        wpq = sb("wpq", [128, 2, DIM])
        taps_m = sb("taps_m", [128, 2, TAPS, 128])
        pick = sb("pick", [128, 4, 8, 128], F32R)
        warm = sb("warm", [128, 512], mybir.dt.bfloat16)
        pad = sb("pad", [128, 5, PADDED, PADDED])
        conv = sb("conv", [128, 2, TOK])
        sq = sb("sq", [128, 5, TOK])
        lnl = sb("lnl", [128, 5, TOK])
        rstd = sb("rstd", [128, 5, TOK])
        nrm = sb("nrm", [128, 5, TOK])
        full = sb("full", [128, 5, TOK])
        hi = sb("hi", [128, 3, TOK], F32R)
        lo = sb("lo", [128, 3, TOK], F32R)
        qs = sb("qs", [128, HEADS, TOK], F32R)
        ks = sb("ks", [128, HEADS, TOK], F32R)
        mx = sb("mx", [128, HEADS, QT], F32R)
        mt = sb("mt", [128, HG, TOK], F32R)
        pt = sb("pt", [128, HEADS, QT, TOK])
        va = sb("va", [128, QT, HEADS, 32])
        os_ = sb("os_", [128, HG, TOK])
        slog = sb("slog", [128, HG, TOK])
        srec = sb("srec", [128, HG, TOK])
        on = sb("on", [128, HG, TOK])

        bank = [ctx.enter_context(nc.psum_tensor(f"bank{i}", [128, 512], F32)) for i in range(8)]

        qkv_ps = [bank[i][:, 0:TOK] for i in range(5)]
        cen_ps = {t: bank[i][:, 0:TOK] for t, i in ((A, 5), (B, 1), (D, 3), (C, 7), (E, 5))}
        var_ps = {t: bank[i][:, 0:TOK] for t, i in ((A, 6), (B, 2), (D, 4), (C, 6), (E, 6))}
        score_banks, key_banks = bank[0:2], bank[2:4]
        o_ps, mt_ps, sum_ps, y_ps = bank[4][:, 0:TOK], bank[5][0:4, 0:TOK], bank[6][:, 0:TOK], bank[7]
        v_ps, misc_ps = bank[7], bank[7]

        ident = cst[:, ID0:ID0 + 128]
        centre = cst[:, CEN0:CEN0 + 128]
        average = cst[:, AVG0:AVG0 + 128]
        group_avg = vec[0:HALF, GRP0:GRP0 + HALF]
        sum_sel = cst[:, SUM0:SUM0 + 128]
        hot = cst[0:64, HOT0:HOT0 + TOK]

        d_x, d_w0, d_cst, d_vec, d_w1 = map(sem, ("d_x", "d_w0", "d_cst", "d_vec", "d_w1"))
        d_nhot, d_rel, d_lora, d_vb, d_wp, d_wpq = map(sem, ("d_nhot", "d_rel", "d_lora", "d_vb", "d_wp", "d_wpq"))
        d_out = sem("d_out")
        warm_set = sem("warm_set")
        zeroed = sem("zeroed")
        mt_zeroed = sem("mt_zeroed")
        rel_zeroed = sem("rel_zeroed")
        ones_set = sem("ones_set")
        hot_set = sem("hot_set")
        picks_set = sem("picks_set")
        qtaps_set = sem("qtaps_set")
        vtaps_set = sem("vtaps_set")
        rel_hi = sem("rel_hi")
        rel_split = sem("rel_split")
        rel_set = sem("rel_set")
        id_set = sem("id_set")
        lora_t = sem("lora_t")
        lora_c = sem("lora_c")
        lora_w = sem("lora_w")
        w1_set = sem("w1_set")
        padded = sem("padded")
        conv_step = [sem("conv_step_k"), sem("conv_step_d")]
        centred = sem("centred")
        squared = sem("squared")
        varied = sem("varied")
        logged = sem("logged")
        rstd_set = sem("rstd_set")
        scaled = sem("scaled")
        full_set = sem("full_set")
        v_turned = sem("v_turned")
        gn_stat, gn_mom, gn_sq, gn_in = map(sems, ("gn_stat", "gn_mom", "gn_sq", "gn_in"))
        gn_sum, gn_mean, gn_msq, gn_var, gn_log, gn_rstd = map(
            sems, ("gn_sum", "gn_mean", "gn_msq", "gn_var", "gn_log", "gn_rstd"))
        xn_set = sems("xn_set")
        projected = sems("projected")
        v_proj = sem("v_proj")
        hi_set, lo_set = sems("hi_set"), sems("lo_set")
        picked = sems("picked")
        moved_a, moved_d = sems("moved_a"), sems("moved_d")
        rel_done = sems("rel_done")
        rel_h, rel_l = sems("rel_h"), sems("rel_l")
        v_set = sems("v_set")
        scored = sems("scored")
        maxed = sems("maxed")
        max_t = sems("max_t")
        max_c = sems("max_c")
        keyed = sems("keyed")
        exped = sems("exped")
        weighed = sems("weighed")
        o_copied = sems("o_copied")
        summed = sems("summed")
        s_logged, s_rec = sems("s_logged"), sems("s_rec")
        normed = sems("normed")
        y_done = sems("y_done")
        x_set = sems("x_set")

        order0 = [B, A, D, C, E]
        order1 = [A, D, B]
        cen_order = [A, B, D, C, E]
        n_cen = {t: i + 1 for i, t in enumerate(cen_order)}

        place3 = {A: 0, B: 1, D: 2}
        full_order = [A, B, D, C, E]
        n_full = {t: i + 1 for i, t in enumerate(full_order)}

        def rel_bank(r):
            return bank[r % 5]

        def rel_src(r):
            p = 0 if r < 8 else 32
            src = rel_bank(r)[p:p + 32, 0:2 * HEADS * SIDE]
            return src.rearrange("p (h n) -> p h n", h=HEADS) if r < 8 else src.rearrange("p (j n) -> p j n", j=2)

        def rel_dst(r):
            if r < 8:
                return qs[0:32, :, 2 * SIDE * r:2 * SIDE * (r + 1)]
            v = qs[32:64, :, :].rearrange("p h (y x) -> p x (h y)", x=SIDE)
            return v[:, 2 * (r - 8):2 * (r - 8) + 2, :]

        lora_ps = [bank[k][0:HALF, 0:2 * DIM].rearrange("p (t n) -> p t n", t=2) for k in (7, 6)]

        block = ctx.enter_context(nc.Block())

        @block.sync
        def _(sp):
            sp.dma_start(xs[0][:], x_t.rearrange("(t p) n -> p t n", p=HALF)).then_inc(d_x, 16)
            sp.dma_start(w0[:, :, 0:2 * DIM], w_qkv0.rearrange("(t p) n -> p t n", p=HALF)[:, :, 0:2 * DIM]).then_inc(d_w0, 16)
            sp.dma_start(w0[:, :, 2 * DIM:], w_qkv0.rearrange("(t p) n -> p t n", p=HALF)[:, :, 2 * DIM:]).then_inc(d_w0, 16)
            sp.dma_start(relt[64:128, :, :], rel).then_inc(d_rel, 16)
            sp.dma_start(w1[:], w_qkv1.rearrange("(t p) n -> p t n", p=HALF)).then_inc(d_w1, 16)
            sp.dma_start(vb1[:], v_bias1).then_inc(d_vb, 16)
            for t in range(2):
                sp.wait_ge(x_set[1], t + 1)
                sp.dma_start(out_t[t * HALF:(t + 1) * HALF, :], xs[2][:, t, :]).then_inc(d_out, 16)
            sp.wait_ge(d_out, 32)

        @block.gpsimd
        def _(pool):
            pool.memset(warm[:], 0.0).then_inc(warm_set, 1)
            pool.memset(pad[:], 0.0).then_inc(zeroed, 1)
            pool.memset(mt[:].bitcast(F32), 0.0).then_inc(mt_zeroed, 1)
            pool.memset(pick[:].bitcast(F32), 0.0).then_inc(zeroed, 1)
            pool.memset(va[:], 0.0).then_inc(zeroed, 1)
            pool.wait_ge(zeroed, 3)
            pool.memset(va[:, :, :, HD:HD + 1], 1.0).then_inc(ones_set, 1)
            pool.wait_ge(d_cst, 16)
            pool.wait_ge(d_vec, 16)

            def windows(b):
                for k in (2 * b, 2 * b + 1):
                    row = relt_s[64:128, k, 0:1]
                    src = bass.AP(row.tensor, row.offset, [list(row.ap[0]), [1, SIDE], [1, SIDE]])
                    first = 0 if k % 2 == 0 else 32
                    for c in (first, first + 16):
                        pool.tensor_copy(rel_w[64:128, k, :, c:c + 16], src).then_inc(rel_set, 1)

            for k in range(TAPS):
                pool.tensor_scalar(taps_m[:, 1, k, :], centre, vec[:, TAP0 + 9 * C + k:TAP0 + 9 * C + k + 1], None,
                                   ALU.mult).then_inc(vtaps_set, 1)
            pool.wait_ge(rel_split, 1)
            pool.wait_ge(rel_zeroed, 1)
            pool.wait_ge(vtaps_set, TAPS)
            windows(0)
            pool.wait_ge(rel_set, 4)
            for h in range(HEADS):
                pool.tensor_copy(ks[0:64, h, :], hot).then_inc(hot_set, 1)
            pool.wait_ge(hot_set, HEADS)
            windows(1)

        @block.scalar
        def _(act):
            act.preload_act_table_set("natural_log_exp_and_others")
            act.dma_start(vec[:], vectors).then_inc(d_vec, 16)
            act.dma_start(cst[:], consts).then_inc(d_cst, 16)
            act.dma_start(lo_w[:], lora).then_inc(d_lora, 16)
            act.dma_start(nhot[:], neg_hot).then_inc(d_nhot, 16)
            act.dma_start(wp[:], w_proj).then_inc(d_wp, 16)
            act.dma_start(wpq[:], w_proj_q).then_inc(d_wpq, 16)

            def group_rstd(b):
                act.wait_ge(gn_var[b], 1)
                act.activation(glog[:], gvar[:], ACT.Ln).then_inc(gn_log[b], 1)
                act.wait_ge(gn_log[b], 1)
                act.activation(grstd[:], glog[:], ACT.Exp, scale=-0.5).then_inc(gn_rstd[b], 1)

            def q_taps(lo_, hi_):
                act.wait_ge(d_cst, 16)
                act.wait_ge(d_vec, 16)
                for k in range(lo_, hi_):
                    act.activation(taps_m[:, 0, k, :], centre, ACT.Copy,
                                   scale=vec[:, TAP0 + 9 * A + k:TAP0 + 9 * A + k + 1]).then_inc(qtaps_set, 1)

            def tile_stats(t):
                r, n = ROWS[t], n_cen[t]
                act.wait_ge(centred, n)
                act.activation(sq[0:r, t, :], cen_ps[t][0:r], ACT.Square).then_inc(squared, 1)

            def tile_rstd(t):
                r, n = ROWS[t], n_cen[t]
                act.wait_ge(varied, n)
                act.activation(lnl[0:r, t, :], var_ps[t][0:r], ACT.Ln, bias=vec[0:r, MASK + 1:MASK + 2]).then_inc(logged, 1)
                act.wait_ge(logged, n)
                act.activation(rstd[0:r, t, :], lnl[0:r, t, :], ACT.Exp, scale=-0.5).then_inc(rstd_set, 1)

            def move_units(b):
                for kind, dst in ((0, qs), (1, ks)):
                    for u in range(0, 6, 2):
                        act.wait_ge(picked[b], 6 * kind + u + 1)
                        act.activation(dst[64:128, 2 * u:2 * u + 2, :],
                                       bank[u][64:128, :].rearrange("p (h n) -> p h n", h=2), ACT.Copy).then_inc(moved_a[b], 1)

            def rel_units(b, between={}):
                for r in range(16):
                    if r in between:
                        between[r]()
                    act.wait_ge(rel_done[b], r + 1)
                    act.activation(rel_dst(r), rel_src(r), ACT.Copy).then_inc(rel_h[b], 1)

            def group_tail(b, g):
                act.wait_ge(summed[b], g + 1)
                act.activation(slog[:, g, :], sum_ps, ACT.Ln).then_inc(s_logged[b], 1)
                act.wait_ge(s_logged[b], g + 1)
                act.activation(srec[:, g, :], slog[:, g, :], ACT.Exp, scale=-1.0).then_inc(s_rec[b], 1)

            def attention(b):
                for i in range(HEADS + 6):
                    if i >= 6 and (i - 6) % 4 == 0:
                        g = (i - 6) // 4
                        act.wait_ge(max_t[b], g + 1)
                        act.activation(mt[0:4, g, :], mt_ps, ACT.Copy).then_inc(max_c[b], 1)
                    if i >= 6:
                        h = i - 6
                        act.wait_ge(keyed[b], h + 1)
                        act.activation(pt[:, h, :, :], key_banks[h % 2][:, :].rearrange("p (k n) -> p k n", k=QT),
                                       ACT.Exp).then_inc(exped[b], 1)
                    if i in (12, 16):
                        group_tail(b, (i - 12) // 4)
                group_tail(b, 2)

            group_rstd(0)
            act.wait_ge(zeroed, 1)
            for i, t in enumerate(order0):
                r = ROWS[t]
                act.wait_ge(projected[0], i + 1)
                act.wait_ge(d_vec, 16)
                act.activation(pad[0:r, t, 1:1 + SIDE, 1:1 + SIDE],
                               qkv_ps[i][0:r].rearrange("p (a c) -> p a c", a=SIDE), ACT.Identity,
                               bias=vec[0:r, BQKV0 + t:BQKV0 + t + 1]).then_inc(padded, 1)
                if i == 2:
                    act.wait_ge(lora_t, 1)
                    act.activation(lo_t[:], misc_ps[0:16, 0:2 * DIM].rearrange("p (k n) -> p k n", k=2), ACT.Copy).then_inc(lora_c, 1)
                if i < 3:
                    q_taps(3 * i, 3 * i + 3)
            act.wait_ge(zeroed, 2)
            idv = ident.rearrange("p (i c) -> p i c", i=8)
            for v, blocks, scale in ((0, (0, 1), 1.0), (1, (2, 3), 1.0), (2, (0, 2), HD ** -0.5), (3, (1, 3), HD ** -0.5)):
                for k in blocks:
                    act.activation(pick[:, v, :, 64 + 16 * k:80 + 16 * k], idv, ACT.Copy, scale=scale).then_inc(picks_set, 1)
            tile_stats(A)
            tile_rstd(A)
            tile_stats(B)
            tile_stats(D)
            tile_rstd(B)
            tile_rstd(D)
            for i, t in enumerate((A, B, D)):
                act.wait_ge(full_set, n_full[t])
                act.activation(hi[:, i, :], full[:, t, :], ACT.Copy).then_inc(hi_set[0], 1)
            move_units(0)
            rel_units(0, {8: lambda: tile_stats(C), 10: lambda: tile_rstd(C)})
            tile_stats(E)
            tile_rstd(E)
            attention(0)

            group_rstd(1)
            for i, t in enumerate(order1):
                act.wait_ge(projected[1], i + 1)
                act.activation(hi[:, place3[t], :], qkv_ps[i], ACT.Identity,
                               bias=vec[:, BQKV1 + place3[t]:BQKV1 + place3[t] + 1]).then_inc(hi_set[1], 1)
            move_units(1)
            rel_units(1)
            attention(1)

        @block.vector
        def _(dve):
            def group_norm_in(b):
                if b == 0:
                    dve.wait_ge(d_x, 16)
                for t in range(2):
                    if b == 1:
                        dve.wait_ge(x_set[0], t + 1)
                    dve.bn_stats(stats[:, t, :], xs[b][:, t, :]).then_inc(gn_stat[b], 1)
                for t in range(2):
                    dve.wait_ge(gn_stat[b], t + 1)
                    dve.bn_aggr(mom[:, t, :], stats[:, t, :]).then_inc(gn_mom[b], 1)
                dve.wait_ge(gn_mom[b], 2)
                dve.tensor_copy(sums[:, 0, :], mom[:, :, 0]).then_inc(gn_sq[b], 1)
                dve.tensor_tensor(sums[:, 1, :], mom[:, :, 0], mom[:, :, 0], ALU.mult).then_inc(gn_sq[b], 1)
                dve.wait_ge(gn_sq[b], 2)
                dve.tensor_tensor(sums[:, 1, :], sums[:, 1, :], mom[:, :, 1], ALU.add).then_inc(gn_in[b], 1)

            def group_norm_out(b):
                dve.wait_ge(gn_sum[b], 1)
                dve.tensor_copy(gmean[:], misc_ps[0:HALF, 0:4].rearrange("p (k t) -> p k t", k=2)).then_inc(gn_mean[b], 1)
                dve.wait_ge(gn_mean[b], 1)
                dve.tensor_tensor(gvar[:], gmean[:, 0, :], gmean[:, 0, :], ALU.mult).then_inc(gn_msq[b], 1)
                dve.wait_ge(gn_msq[b], 1)
                dve.scalar_tensor_tensor(out=gvar[:], in0=gmean[:, 1, :], scalar=EPS, in1=gvar[:],
                                         op0=ALU.add, op1=ALU.subtract).then_inc(gn_var[b], 1)
                dve.wait_ge(gn_rstd[b], 1)
                for t in range(2):
                    dve.tensor_scalar(xn[:, t, :], xs[b][:, t, :], gmean[:, 0, t:t + 1], grstd[:, t:t + 1],
                                      ALU.subtract, ALU.mult).then_inc(xn_set[b], 1)

            def normalise(t):
                r, n = ROWS[t], n_cen[t]
                dve.wait_ge(rstd_set, n)
                dve.tensor_tensor(nrm[0:r, t, :], cen_ps[t][0:r], rstd[0:r, t, :], ALU.mult).then_inc(scaled, 1)
                dve.wait_ge(scaled, n)
                dve.tensor_scalar(full[0:r, t, :], nrm[0:r, t, :], vec[0:r, LNG0 + t:LNG0 + t + 1],
                                  vec[0:r, LNB0 + t:LNB0 + t + 1], ALU.mult, ALU.add).then_inc(full_set, 1)

            def move_units(b):
                for kind, dst in ((0, qs), (1, ks)):
                    for u in range(1, 6, 2):
                        dve.wait_ge(picked[b], 6 * kind + u + 1)
                        dve.tensor_copy(dst[64:128, 2 * u:2 * u + 2, :],
                                        bank[u][64:128, :].rearrange("p (h n) -> p h n", h=2)).then_inc(moved_d[b], 1)

            def rel_units(b, between={}):
                for r in range(16):
                    if r in between:
                        between[r]()
                    p = 0 if r < 8 else 32
                    dve.wait_ge(rel_h[b], r + 1)
                    dve.scalar_tensor_tensor(out=rel_dst(r), in0=rel_dst(r).bitcast(F32), scalar=vec[p:p + 32, MASK:MASK + 1],
                                             in1=rel_src(r), op0=ALU.mult, op1=ALU.add).then_inc(rel_l[b], 1)

            def o_copy(b, g):
                dve.wait_ge(weighed[b], g + 1)
                dve.tensor_copy(os_[:, g, :], o_ps).then_inc(o_copied[b], 1)

            def o_norm(b, g):
                dve.wait_ge(s_rec[b], g + 1)
                dve.tensor_tensor(on[:, g, :], os_[:, g, :], srec[:, g, :], ALU.mult).then_inc(normed[b], 1)

            def attention(b):
                for h in range(HEADS):
                    dve.wait_ge(scored[b], h + 1)
                    dve.tensor_reduce(mx[:, h, :], score_banks[h % 2][:, :].rearrange("p (q n) -> p q n", q=QT),
                                      AXX, ALU.max).then_inc(maxed[b], 1)
                    if h == 11:
                        o_copy(b, 0)
                o_norm(b, 0)
                o_copy(b, 1)
                o_norm(b, 1)
                o_copy(b, 2)
                o_norm(b, 2)
                dve.wait_ge(y_done[b], 1)
                for t in range(2):
                    dve.scalar_tensor_tensor(out=xs[b + 1][:, t, :], in0=y_ps[0:HALF, t * TOK:(t + 1) * TOK],
                                             scalar=vec[0:HALF, BPROJ + 2 * b + t:BPROJ + 2 * b + t + 1],
                                             in1=xs[b][:, t, :], op0=ALU.add, op1=ALU.add).then_inc(x_set[b], 1)

            dve.memset(rel_w[:].bitcast(F32), 0.0).then_inc(rel_zeroed, 1)
            group_norm_in(0)
            group_norm_out(0)
            dve.wait_ge(d_cst, 16)
            dve.wait_ge(d_vec, 16)
            dve.wait_ge(d_nhot, 16)
            dve.tensor_copy(ident_r[:], ident).then_inc(id_set, 1)
            dve.tensor_copy(nhot_r[:], nhot[:].rearrange("p (j n) -> p j n", j=4)).then_inc(id_set, 1)
            dve.wait_ge(d_rel, 16)
            dve.tensor_copy(relt_hi[64:128], relt[64:128]).then_inc(rel_hi, 1)
            dve.wait_ge(rel_hi, 1)
            dve.scalar_tensor_tensor(out=relt_s[64:128].rearrange("p a b -> p (a b)"),
                                     in0=relt_hi[64:128].bitcast(F32).rearrange("p a b -> p (a b)"),
                                     scalar=vec[64:128, MASK:MASK + 1],
                                     in1=relt[64:128].rearrange("p a b -> p (a b)"),
                                     op0=ALU.mult, op1=ALU.add).then_inc(rel_split, 1)
            for k in range(TAPS):
                if k == 4:
                    dve.wait_ge(d_w1, 16)
                    dve.wait_ge(lora_w, 1)
                    for n, col in ((0, 0), (1, 2 * DIM)):
                        for_w = w1[:, :, col:col + DIM]
                        dve.tensor_tensor(for_w, lora_ps[n], for_w, ALU.add).then_inc(w1_set, 1)
                for s, t in enumerate((B, D)):
                    if k == 0:
                        dve.wait_ge(padded, order0.index(t) + 1)
                    src = pad[:, t, k // 3:k // 3 + SIDE, k % 3:k % 3 + SIDE]
                    dst = conv[:, s, :].rearrange("p (a c) -> p a c", a=SIDE)
                    w = vec[:, TAP0 + 9 * t + k:TAP0 + 9 * t + k + 1]
                    if k == 0:
                        dve.tensor_scalar(dst, src, w, None, ALU.mult).then_inc(conv_step[s], 1)
                    else:
                        dve.wait_ge(conv_step[s], k)
                        dve.scalar_tensor_tensor(out=dst, in0=src, scalar=w, in1=dst, op0=ALU.mult,
                                                 op1=ALU.add).then_inc(conv_step[s], 1)
            normalise(A)
            normalise(B)
            normalise(D)
            for i, t in enumerate((A, B, D)):
                dve.wait_ge(hi_set[0], i + 1)
                dve.tensor_tensor(lo[:, i, :], full[:, t, :], hi[:, i, :].bitcast(F32), ALU.subtract).then_inc(lo_set[0], 1)
            move_units(0)

            def v_to_tokens(part, h0, h1):
                dve.wait_ge(ones_set, 1)
                dve.wait_ge(v_turned, part)
                dve.tensor_copy(va[:, :, h0:h1, 0:HD],
                                v_ps[:, 0:QT * HD * (h1 - h0)].rearrange("p (q h c) -> p q h c", q=QT, c=HD)).then_inc(v_set[0], 1)

            rel_units(0, {12: lambda: normalise(C), 15: lambda: v_to_tokens(1, 0, 8)})
            normalise(E)
            v_to_tokens(2, 8, 12)
            attention(0)

            group_norm_in(1)
            group_norm_out(1)
            for i, t in enumerate(order1):
                dve.wait_ge(hi_set[1], i + 1)
                dve.scalar_tensor_tensor(out=lo[:, place3[t], :], in0=qkv_ps[i],
                                         scalar=vec[:, BQKV1 + place3[t]:BQKV1 + place3[t] + 1],
                                         in1=hi[:, place3[t], :].bitcast(F32), op0=ALU.add, op1=ALU.subtract).then_inc(lo_set[1], 1)
            move_units(1)
            rel_units(1)
            dve.wait_ge(d_vb, 16)
            dve.wait_ge(v_proj, 1)
            for q in range(QT):
                dve.tensor_tensor(va[:, q, :, 0:HD],
                                  bank[7][:, q * DIM:(q + 1) * DIM].rearrange("p (h c) -> p h c", h=HEADS),
                                  vb1[:].rearrange("p (h c) -> p h c", h=HEADS), ALU.add).then_inc(v_set[1], 1)
            attention(1)

        @block.tensor
        def _(pe):
            def warm_up(n):
                for _ in range(n):
                    pe.matmul(bank[5][:, :], warm[:, 0:128], warm[:, :], start=True, stop=True)

            def group_sums(b):
                pe.wait_ge(gn_in[b], 1)
                pe.wait_ge(gn_sq[b], 2)
                if b == 0:
                    pe.wait_ge(d_vec, 16)
                pe.matmul(misc_ps[0:HALF, 0:4], group_avg, sums[:].rearrange("p k t -> p (k t)"),
                          start=True, stop=True).then_inc(gn_sum[b], 1)

            def project(b, i, t, w):
                for n, (p, col, width) in enumerate(PARTS[t]):
                    for k in range(2):
                        mm = pe.matmul(qkv_ps[i][p:p + width, :], w[:, k, col:col + width], xn[:, k, :],
                                       start=(k == 0), stop=(k == 1))
                mm.then_inc(projected[b], 1)

            def convolve(t, v, first, last):
                r = ROWS[t]
                if first == 0:
                    pe.wait_ge(qtaps_set if v == 0 else vtaps_set, TAPS)
                    pe.wait_ge(padded, order0.index(t) + 1)
                for k in range(first, last):
                    mm = pe.matmul(cen_ps[t][0:r, :], taps_m[0:r, v, k, 0:r],
                                   pad[0:r, t, k // 3:k // 3 + SIDE, k % 3:k % 3 + SIDE],
                                   start=(k == 0), stop=(k == TAPS - 1))
                    if k == TAPS - 1:
                        mm.then_inc(centred, 1)

            def variance(t):
                r = ROWS[t]
                pe.wait_ge(squared, n_cen[t])
                if t == A:
                    pe.wait_ge(w1_set, 2)
                if t == C:
                    pe.wait_ge(logged, n_cen[A])
                if t == E:
                    pe.wait_ge(logged, n_cen[C])
                pe.matmul(var_ps[t][0:r, :], average[0:r, 0:r], sq[0:r, t, :], start=True, stop=True).then_inc(varied, 1)

            def turn(t):
                r, col = ROWS[t], 0
                if t == E:
                    pe.wait_ge(v_set[0], 1)
                pe.wait_ge(full_set, n_full[t])
                for q in range(QT):
                    mm = pe.transpose(v_ps[:, col + q * r:col + (q + 1) * r], full[0:r, t, q * 128:(q + 1) * 128],
                                      ident[0:r, 0:r])
                mm.then_inc(v_turned, 1)

            def pick_units(b):
                for kind, place, v in ((0, q_place, 0), (1, k_place, 2)):
                    for u in range(6):
                        if kind == 0:
                            pe.wait_ge(lo_set[b], 3)
                        elif u % 2 == 0:
                            pe.wait_ge(moved_a[b], u // 2 + 1)
                        else:
                            pe.wait_ge(moved_d[b], u // 2 + 1)
                        for j in range(2):
                            t, i = place(2 * u + j)
                            dst = bank[u][:, j * TOK:(j + 1) * TOK]
                            pe.matmul(dst, pick[:, v, i, :], hi[:, place3[t], :], start=True, stop=False)
                            mm = pe.matmul(dst, pick[:, v + 1, i, :], lo[:, place3[t], :], start=False, stop=True)
                        mm.then_inc(picked[b], 1)

            def rel_units(b, between={}):
                pe.wait_ge(rel_set, 4 * b + 4)
                for r in range(16):
                    if r < 5:
                        pe.wait_ge(moved_a[b], 3 + (r // 2 + 1 if r % 2 == 0 else 0))
                        pe.wait_ge(moved_d[b], 3 + (r // 2 + 1 if r % 2 == 1 else 0))
                    else:
                        pe.wait_ge(rel_l[b], r - 4)
                    for j in range(2):
                        if r < 8:
                            y = 2 * r + j
                            mm = pe.matmul(rel_bank(r)[0:32, 0:2 * HEADS * SIDE].rearrange("p (h j n) -> p j h n", j=2, n=SIDE)[:, j],
                                           rel_w[64:128, 2 * b, SIDE - 1 - y, 0:32],
                                           qs[64:128, :, y * SIDE:(y + 1) * SIDE], start=True, stop=True)
                        else:
                            x = 2 * (r - 8) + j
                            mm = pe.matmul(rel_bank(r)[0:64, j * HEADS * SIDE:(j + 1) * HEADS * SIDE],
                                           rel_w[64:128, 2 * b + 1, SIDE - 1 - x, 0:64],
                                           qs[64:128, :, :].rearrange("p h (y x) -> p x (h y)", x=SIDE)[:, x],
                                           start=True, stop=True)
                    mm.then_inc(rel_done[b], 1)
                    if r in between:
                        between[r]()

            def score(b, h):
                if h == 0:
                    pe.wait_ge(rel_l[b], 16)
                    pe.wait_ge(moved_a[b], 6)
                    pe.wait_ge(moved_d[b], 6)
                    pe.wait_ge(hot_set, HEADS)
                if h >= 2:
                    pe.wait_ge(maxed[b], h - 1)
                for q in range(QT):
                    mm = pe.matmul(score_banks[h % 2][:, q * TOK:(q + 1) * TOK], qs[:, h, q * 128:(q + 1) * 128], ks[:, h, :],
                                   start=True, stop=True)
                mm.then_inc(scored[b], 1)

            def turn_maxima(b, g):
                pe.wait_ge(maxed[b], 4 * g + 4)
                if b == 0:
                    pe.wait_ge(full_set, 5)
                    pe.wait_ge(mt_zeroed, 1)
                pe.wait_ge(id_set, 2)
                if g >= 1:
                    pe.wait_ge(max_c[b], g)
                for q in range(QT):
                    mm = pe.matmul(mt_ps[:, q * 128:(q + 1) * 128], mx[:, 4 * g:4 * g + 4, q], ident_r[:],
                                   start=True, stop=True)
                mm.then_inc(max_t[b], 1)

            def score_by_key(b, h):
                g, j = h // 4, h % 4
                pe.wait_ge(max_c[b], g + 1)
                if h >= 2:
                    pe.wait_ge(exped[b], h - 1)
                for k in range(QT):
                    dst = key_banks[h % 2][:, k * TOK:(k + 1) * TOK]
                    pe.matmul(dst, ks[:, h, k * 128:(k + 1) * 128], qs[:, h, :], start=True, stop=False)
                    mm = pe.matmul(dst, nhot_r[:, j, :], mt[:, g, :], start=False, stop=True)
                mm.then_inc(keyed[b], 1)

            def weigh(b, g):
                pe.wait_ge(exped[b], 4 * g + 4)
                pe.wait_ge(v_set[b], 2)
                if g >= 1:
                    pe.wait_ge(o_copied[b], g)
                for k in range(QT):
                    for j in range(4):
                        mm = pe.matmul(o_ps[32 * j:32 * j + 32, :], va[:, k, 4 * g + j, :], pt[:, 4 * g + j, k, :],
                                       start=(k == 0), stop=(k == QT - 1), skip_group_check=True)
                mm.then_inc(weighed[b], 1)

            def spread_sums(b, g):
                pe.wait_ge(o_copied[b], g + 1)
                if g >= 1:
                    pe.wait_ge(s_logged[b], g)
                pe.matmul(sum_ps, sum_sel, os_[:, g, :], start=True, stop=True).then_inc(summed[b], 1)

            first_y = [True, True]

            def out_project(b, g):
                pe.wait_ge(normed[b], g + 1)
                for t in range(2):
                    mm = pe.matmul(y_ps[0:HALF, t * TOK:(t + 1) * TOK], wp[:, b, g, t * HALF:(t + 1) * HALF], on[:, g, :],
                                   start=first_y[b], stop=(g == 2), skip_group_check=True)
                    first_y[b] = False
                if g == 2:
                    mm.then_inc(y_done[b], 1)

            def q_project():
                for t in range(2):
                    for k, (tile, r) in enumerate(((A, 128), (D, 64))):
                        pe.matmul(y_ps[0:HALF, t * TOK:(t + 1) * TOK], wpq[0:r, k, t * HALF:(t + 1) * HALF], full[0:r, tile, :],
                                  start=first_y[0], stop=False, skip_group_check=True)
                        first_y[0] = False

            def attention(b):
                for i in range(HEADS + 6):
                    if i < HEADS:
                        score(b, i)
                    if i >= 5 and (i - 5) % 4 == 0:
                        turn_maxima(b, (i - 5) // 4) if i < 14 else None
                    if i == 12:
                        pe.wait_ge(d_wp, 16)
                        if b == 0:
                            pe.wait_ge(d_wpq, 16)
                            q_project()
                    if i >= 6:
                        score_by_key(b, i - 6)
                    if i in (11, 15):
                        weigh(b, (i - 11) // 4)
                    if i in (12, 16):
                        spread_sums(b, (i - 12) // 4)
                out_project(b, 0)
                weigh(b, 2)
                out_project(b, 1)
                spread_sums(b, 2)
                out_project(b, 2)

            pe.wait_ge(warm_set, 1)
            warm_up(WARM0)
            group_sums(0)
            warm_up(WARM1)
            pe.wait_ge(xn_set[0], 2)
            pe.wait_ge(d_w0, 32)
            for i, t in enumerate(order0):
                project(0, i, t, w0)
                if i == 2:
                    pe.wait_ge(d_lora, 16)
                    for k in range(2):
                        mm = pe.matmul(misc_ps[0:16, k * DIM:(k + 1) * DIM], lo_w[:, 2 * DIM + 16 * k:2 * DIM + 16 * k + 16],
                                       lo_w[:, 0:DIM], start=True, stop=True)
                    mm.then_inc(lora_t, 1)
            pe.wait_ge(lora_c, 1)
            for k in range(2):
                for t in range(2):
                    mm = pe.matmul(lora_ps[k][:, t, :], lo_t[:, k, t * HALF:(t + 1) * HALF], lo_w[:, DIM:2 * DIM],
                                   start=True, stop=True)
            mm.then_inc(lora_w, 1)
            convolve(A, 0, 0, TAPS)
            variance(A)
            convolve(C, 1, 0, 5)
            for s, t in enumerate((B, D)):
                pe.wait_ge(conv_step[s], TAPS)
                pe.wait_ge(padded, 5)
                pe.matmul(cen_ps[t], centre, conv[:, s, :], start=True, stop=True).then_inc(centred, 1)
            variance(B)
            variance(D)
            pick_units(0)

            def e_taps(first, last):
                if first == 0:
                    pe.wait_ge(moved_d[0], 6)
                convolve(E, 1, first, last)

            def c_end():
                convolve(C, 1, 7, TAPS)

            rel_units(0, {0: lambda: convolve(C, 1, 5, 6), 1: lambda: convolve(C, 1, 6, 7), 2: c_end,
                          5: lambda: e_taps(0, 1), 6: lambda: e_taps(1, 2), 7: lambda: e_taps(2, 3),
                          8: lambda: variance(C), 9: lambda: e_taps(3, 5), 10: lambda: e_taps(5, 6),
                          11: lambda: e_taps(6, 7), 12: lambda: e_taps(7, 8), 13: lambda: e_taps(8, 9),
                          14: lambda: turn(C)})
            variance(E)
            turn(E)
            attention(0)

            group_sums(1)
            pe.wait_ge(xn_set[1], 2)
            for i, t in enumerate(order1):
                project(1, i, t, w1)
            for q in range(QT):
                for k in range(2):
                    mm = pe.matmul(bank[7][:, q * DIM:(q + 1) * DIM], xn[:, k, q * 128:(q + 1) * 128],
                                   w1[:, k, 2 * DIM:3 * DIM], start=(k == 0), stop=(k == 1))
            mm.then_inc(v_proj, 1)
            pick_units(1)
            rel_units(1)
            pe.wait_ge(v_set[1], 2)
            attention(1)


def shape_constants(np):
    cst = np.zeros((128, NCST), np.float32)
    r = np.arange(128)
    same = (r[:, None] // HD == r[None, :] // HD).astype(np.float32) / HD
    cst[:, ID0:ID0 + 128] = np.eye(128, dtype=np.float32)
    cst[:, CEN0:CEN0 + 128] = np.eye(128, dtype=np.float32) - same
    cst[:, AVG0:AVG0 + 128] = same
    c = np.arange(HALF)
    vec = np.zeros((128, NVEC), np.float32)
    vec[:HALF, GRP0:GRP0 + HALF] = (c[:, None] // GROUP == c[None, :] // GROUP) / np.float32(GROUP)
    cst[:, SUM0:SUM0 + 128] = r[:, None] == r[None, :] // 32 * 32 + HD
    t = np.arange(TOK)
    for k in range(SIDE):
        for b in range(2):
            cst[16 * b + k, HOT0:HOT0 + TOK] = t // SIDE == k
            cst[32 + 16 * b + k, HOT0:HOT0 + TOK] = t % SIDE == k
    hot = np.zeros((128, 4, 128), np.float32)
    for j in range(4):
        hot[j, j] = -1.0
    return cst, hot.reshape(128, 512), vec


def kernel(**inputs):
    import numpy as np
    import concourse.bacc as bacc
    from concourse.bass_utils import run_bass_kernel_spmd

    a = {k: np.asarray(v) for k, v in inputs.items()}
    cst, hot, vec = shape_constants(np)
    kind = {A: "q", B: "k", C: "v", E: "v"}
    for t, parts in PARTS.items():
        for n, (p, col, width) in enumerate(parts):
            name = "qk"[n] if t == D else kind[t]
            rep = width // HD
            taps = a[f"L0_conv_w_pool_{name}"].reshape(TAPS, HD)
            vec[p:p + width, TAP0 + 9 * t:TAP0 + 9 * t + TAPS] = np.tile(taps.T, (rep, 1))
            vec[p:p + width, BQKV0 + t] = a["L0_conv_b_qkv"][col:col + width]
            vec[p:p + width, LNG0 + t] = np.tile(a[f"L0_conv_g_{name}"], rep)
            vec[p:p + width, LNB0 + t] = np.tile(a[f"L0_conv_b_{name}"], rep)
            if t in (A, B, D):
                vec[p:p + width, BQKV1 + {A: 0, B: 1, D: 2}[t]] = a["L1_conv_qkv_b"][col:col + width]
    for b, name in enumerate(("L0_conv_b_proj", "L1_conv_proj_b")):
        vec[:HALF, BPROJ + 2 * b:BPROJ + 2 * b + 2] = a[name].reshape(2, HALF).T
    vec[:, MASK] = -(np.arange(128) // HD % 2)
    vec[:, MASK + 1] = EPS

    rel = np.zeros((64, 4, REL), np.float32)
    for k, name in enumerate(("L0_conv_rel_pos_h", "L0_conv_rel_pos_w", "L1_conv_rel_pos_h", "L1_conv_rel_pos_w")):
        rel[:, k] = np.tile(a[name][REL - 1::-1].T, (4, 1))
    lora = np.concatenate([a["L1_conv_FacTu_w"].T, a["L1_conv_FacTv_w"], a["L1_conv_q_facts_w"], a["L1_conv_v_facts_w"]], 1)
    w_proj = np.zeros((HG, 4, 32, 2, DIM), np.float32)
    w_t = a["L0_conv_w_proj"].T
    w_proj[:, :, :HD, 0] = w_t.reshape(HG, 4, HD, DIM)
    w_proj[:, :, :HD, 1] = a["L1_conv_proj_w"].reshape(HG, 4, HD, DIM)
    w_proj = w_proj.reshape(HG, 128, 2, DIM).transpose(1, 2, 0, 3)
    w_proj_q = np.zeros((128, 2, DIM), np.float32)
    w_proj_q[:, 0] = w_t[:128]
    w_proj_q[:64, 1] = w_t[128:]
    arrays = {
        "x_t": a["x"].reshape(TOK, DIM).T, "w_qkv0": a["L0_conv_w_qkv"].T, "w_qkv1": a["L1_conv_qkv_w"],
        "consts": cst, "vectors": vec, "neg_hot": hot, "rel": rel, "lora": lora,
        "v_bias1": np.broadcast_to(a["L1_conv_qkv_b"][2 * DIM:], (128, DIM)),
        "w_proj": w_proj, "w_proj_q": w_proj_q,
    }
    arrays = {k: np.ascontiguousarray(v) for k, v in arrays.items()}
    nc = bacc.Bacc("TRN2", target_bir_lowering=False, num_devices=1)
    args = [nc.dram_tensor(k, v.shape, F32, kind="ExternalInput").ap() for k, v in arrays.items()]
    out = nc.dram_tensor("out_t", (DIM, TOK), F32, kind="ExternalOutput").ap()
    attention_blocks(nc, *args, out)
    r = run_bass_kernel_spmd(nc, [arrays], core_ids=[0])
    y = r.results[0]["out_t"]
    return np.ascontiguousarray(y.T).reshape(1, SIDE, SIDE, DIM)
```

```python
from contextlib import ExitStack

import concourse.bass as bass
from concourse import mybir

F32 = mybir.dt.float32
F32R = mybir.dt.float32r
ALU = mybir.AluOpType
ACT = mybir.ActivationFunctionType
AXX = mybir.AxisListType.X

SIDE = 16
TOK = SIDE * SIDE
DIM = 192
HEADS = 12
HD = DIM // HEADS
HALF = DIM // 2
GROUP = 6
QT = TOK // 128
HG = HEADS // 4
REL = 2 * SIDE - 1
PADDED = SIDE + 2
TAPS = 9
EPS = 1e-5
WARM0, WARM1 = 9, 3

A, B, D, C, E = range(5)
PARTS = {
    A: [(0, 0, 128)],
    B: [(0, DIM, 128)],
    D: [(0, 128, 64), (64, DIM + 128, 64)],
    C: [(0, 2 * DIM, 128)],
    E: [(0, 2 * DIM + 128, 64)],
}
ROWS = {A: 128, B: 128, D: 128, C: 128, E: 64}

ID0, CEN0, AVG0, SUM0 = 0, 128, 256, 384
NCST = SUM0 + 128
TAP0, BQKV0, LNG0, LNB0, BQKV1, BPROJ, MASK = 0, 45, 50, 55, 60, 63, 67
GRP0 = 69
NVEC = GRP0 + HALF


def q_place(h):
    return (A, h) if h < 8 else (D, h - 8)


def k_place(h):
    return (B, h) if h < 8 else (D, h - 4)


def attention_blocks(nc, x_t, w_qkv0, w_qkv1, consts, hots, vectors, neg_hot, rel, lora, v_bias1, w_proj, w_proj_q, out_t):
    with ExitStack() as ctx:
        def sb(name, shape, dt=F32):
            return ctx.enter_context(nc.sbuf_tensor(name, shape, dt))

        def sem(name):
            return ctx.enter_context(nc.semaphore(name))

        def sems(name):
            return [sem(f"{name}_{b}") for b in range(2)]

        xs = [sb(f"x_{i}", [HALF, 2, TOK]) for i in range(3)]
        xn = sb("xn", [HALF, 2, TOK])
        stats = sb("stats", [HALF, 2, 6])
        mom = sb("mom", [HALF, 2, 2])
        sums = sb("sums", [HALF, 2, 2])
        gmean = sb("gmean", [HALF, 2, 2])
        gvar = sb("gvar", [HALF, 2])
        glog = sb("glog", [HALF, 2])
        grstd = sb("grstd", [HALF, 2])
        w0 = sb("w0", [HALF, 2, 3 * DIM])
        w1 = sb("w1", [HALF, 2, 3 * DIM])
        cst = sb("cst", [128, NCST])
        vec = sb("vec", [128, NVEC])
        nhot = sb("nhot", [128, 4 * 128])
        nhot_r = sb("nhot_r", [128, 4, 128], F32R)
        ident_r = sb("ident_r", [128, 128], F32R)
        relt = sb("relt", [128, 4, REL])
        relt_hi = sb("relt_hi", [128, 4, REL], F32R)
        relt_s = sb("relt_s", [128, 4, REL])
        rel_w = sb("rel_w", [128, 4, SIDE, 64], F32R)
        lo_w = sb("lo_w", [16, 2 * DIM + 32])
        lo_t = sb("lo_t", [16, 2, DIM])
        vb1 = sb("vb1", [128, DIM])
        wp = sb("wp", [128, 2, HG, DIM])
        wpq = sb("wpq", [128, 2, DIM])
        taps_m = sb("taps_m", [128, 2, TAPS, 128])
        pick = sb("pick", [128, 4, 8, 128], F32R)
        warm = sb("warm", [128, 512], mybir.dt.bfloat16)
        pad = sb("pad", [128, 5, PADDED, PADDED])
        conv = sb("conv", [128, 2, TOK])
        sq = sb("sq", [128, 5, TOK])
        lnl = sb("lnl", [128, 5, TOK])
        rstd = sb("rstd", [128, 5, TOK])
        nrm = sb("nrm", [128, 5, TOK])
        full = sb("full", [128, 5, TOK])
        hi = sb("hi", [128, 3, TOK], F32R)
        lo = sb("lo", [128, 3, TOK], F32R)
        qs = sb("qs", [128, HEADS, TOK], F32R)
        ks = sb("ks", [128, HEADS, TOK], F32R)
        mx = sb("mx", [128, HEADS, QT], F32R)
        mt = sb("mt", [128, HG, TOK], F32R)
        pt = sb("pt", [128, HEADS, QT, TOK])
        ones = sb("ones", [128, 32])
        va = sb("va", [128, QT, HEADS, 32])
        os_ = sb("os_", [128, HG, TOK])
        slog = sb("slog", [128, HG, TOK])
        srec = sb("srec", [128, HG, TOK])
        on = sb("on", [128, HG, TOK])

        bank = [ctx.enter_context(nc.psum_tensor(f"bank{i}", [128, 512], F32)) for i in range(8)]

        ring = [bank[0], bank[1], bank[6]]
        key_banks = bank[2:4]
        o_ps, mt_ps, sum_ps, y_ps = bank[4][:, 0:TOK], bank[5][0:4, 0:TOK], bank[5][:, 0:TOK], bank[7]
        qkv_ps = [bank[i][:, 0:TOK] for i in range(5)]
        qkv1_ps = [bank[i][:, 0:TOK] for i in (0, 3, 2)]
        cen_ps = {t: bank[i][:, 0:TOK] for t, i in ((A, 0), (B, 5), (C, 2), (D, 7), (E, 5))}
        var_ps = {t: bank[i][:, 0:TOK] for t, i in ((A, 1), (B, 6), (C, 3), (D, 4), (E, 4))}
        turn_ps, misc_ps = bank[4], bank[7]

        ident = cst[:, ID0:ID0 + 128]
        centre = cst[:, CEN0:CEN0 + 128]
        average = cst[:, AVG0:AVG0 + 128]
        group_avg = vec[0:HALF, GRP0:GRP0 + HALF]
        sum_sel = cst[:, SUM0:SUM0 + 128]

        d_x, d_w0, d_cst, d_vec, d_w1 = map(sem, ("d_x", "d_w0", "d_cst", "d_vec", "d_w1"))
        d_nhot, d_rel, d_lora, d_vb, d_wp, d_wpq = map(sem, ("d_nhot", "d_rel", "d_lora", "d_vb", "d_wp", "d_wpq"))
        d_hot = sem("d_hot")
        d_out = sem("d_out")
        warm_set = sem("warm_set")
        zeroed = sem("zeroed")
        mt_zeroed = sem("mt_zeroed")
        rel_zeroed = sem("rel_zeroed")
        ones_set = sem("ones_set")
        picks_set = sem("picks_set")
        qtaps_set = sem("qtaps_set")
        vtaps_set = sem("vtaps_set")
        rel_hi = sem("rel_hi")
        rel_split = sem("rel_split")
        rel_set = sem("rel_set")
        id_set = sem("id_set")
        lora_t = sem("lora_t")
        lora_c = sem("lora_c")
        lora_w = sem("lora_w")
        w1_set = sem("w1_set")
        padded = sem("padded")
        conv_step = [sem("conv_step_k"), sem("conv_step_d")]
        centred = sem("centred")
        squared = sem("squared")
        varied = sem("varied")
        logged = sem("logged")
        rstd_set = sem("rstd_set")
        scaled = sem("scaled")
        full_set = sem("full_set")
        v_turned = sem("v_turned")
        gn_stat, gn_mom, gn_sq, gn_in = map(sems, ("gn_stat", "gn_mom", "gn_sq", "gn_in"))
        gn_sum, gn_mean, gn_msq, gn_var, gn_log, gn_rstd = map(
            sems, ("gn_sum", "gn_mean", "gn_msq", "gn_var", "gn_log", "gn_rstd"))
        xn_set = sems("xn_set")
        projected = sems("projected")
        v_proj = sem("v_proj")
        hi_set, lo_set = sems("hi_set"), sems("lo_set")
        picked = sems("picked")
        moved_a, moved_d = sems("moved_a"), sems("moved_d")
        rel_done = sems("rel_done")
        rel_h, rel_l = sems("rel_h"), sems("rel_l")
        v_set = sems("v_set")
        scored = sems("scored")
        maxed = sems("maxed")
        max_t = sems("max_t")
        max_c = sems("max_c")
        keyed = sems("keyed")
        exped = sems("exped")
        weighed = sems("weighed")
        o_copied = sems("o_copied")
        summed = sems("summed")
        s_logged, s_rec = sems("s_logged"), sems("s_rec")
        normed = sems("normed")
        y_done = sems("y_done")
        x_set = sems("x_set")

        order0 = [A, B, C, D, E]
        order1 = [A, B, D]
        cen_order = [A, B, C, E, D]
        n_cen = {t: i + 1 for i, t in enumerate(cen_order)}

        place3 = {A: 0, B: 1, D: 2}
        n_padded = {t: i + 1 for i, t in enumerate(order0)}

        def unit_rel_dst(g, r):
            return qs[0:64, 4 * g:4 * g + 4, 128 * r:128 * r + 128]

        def ring_bank(g, n):
            return ring[(10 * g + n) % 3]

        def unit_rel_src(g, r):
            return ring_bank(g, 4 + r)[0:64, :].rearrange("p (n h) -> p h n", h=4)

        lora_ps = [bank[k][0:HALF, 0:2 * DIM].rearrange("p (t n) -> p t n", t=2) for k in (7, 3)]

        block = ctx.enter_context(nc.Block())

        @block.sync
        def _(sp):
            sp.dma_start(xs[0][:], x_t.rearrange("(t p) n -> p t n", p=HALF)).then_inc(d_x, 16)
            sp.dma_start(w0[:, :, 0:2 * DIM], w_qkv0.rearrange("(t p) n -> p t n", p=HALF)[:, :, 0:2 * DIM]).then_inc(d_w0, 16)
            sp.dma_start(w0[:, :, 2 * DIM:], w_qkv0.rearrange("(t p) n -> p t n", p=HALF)[:, :, 2 * DIM:]).then_inc(d_w0, 16)
            sp.dma_start(relt[64:128, :, :], rel).then_inc(d_rel, 16)
            sp.dma_start(w1[:], w_qkv1.rearrange("(t p) n -> p t n", p=HALF)).then_inc(d_w1, 16)
            sp.dma_start(vb1[:], v_bias1).then_inc(d_vb, 16)
            for t in range(2):
                sp.wait_ge(x_set[1], t + 1)
                sp.dma_start(out_t[t * HALF:(t + 1) * HALF, :], xs[2][:, t, :]).then_inc(d_out, 16)
            sp.wait_ge(d_out, 32)

        @block.gpsimd
        def _(pool):
            pool.memset(warm[:], 0.0).then_inc(warm_set, 1)
            pool.memset(pad[:], 0.0).then_inc(zeroed, 1)
            pool.memset(rel_w[:, 1::2, :, 0:32].bitcast(F32), 0.0).then_inc(rel_zeroed, 1)
            hots_again = bass.AP(hots.tensor, hots.offset, [[TOK, 64], [0, HEADS], [1, TOK]])
            pool.wait_ge(d_cst, 16)
            pool.dma_start(ks[0:64], hots_again).then_inc(d_hot, 16)
            pool.memset(pick[:].bitcast(F32), 0.0).then_inc(zeroed, 1)
            pool.memset(ones[:], 1.0)
            pool.memset(va[:], 0.0).then_inc(zeroed, 1)
            pool.wait_ge(zeroed, 3)
            pool.memset(va[:, :, :, HD:HD + 1], 1.0).then_inc(ones_set, 1)
            pool.memset(mt[:].bitcast(F32), 0.0).then_inc(mt_zeroed, 1)
            pool.wait_ge(rel_split, 1)
            pool.wait_ge(mt_zeroed, 1)
            for k in range(4):
                row = relt_s[64:128, k, 0:1]
                src = bass.AP(row.tensor, row.offset, [list(row.ap[0]), [1, SIDE], [1, SIDE]])
                first = 0 if k % 2 == 0 else 32
                for c in (first, first + 16):
                    pool.tensor_copy(rel_w[64:128, k, :, c:c + 16], src).then_inc(rel_set, 1)

        @block.scalar
        def _(act):
            act.preload_act_table_set("natural_log_exp_and_others")
            act.dma_start(vec[:], vectors).then_inc(d_vec, 16)
            act.dma_start(cst[:], consts).then_inc(d_cst, 16)
            act.dma_start(lo_w[:], lora).then_inc(d_lora, 16)
            act.dma_start(nhot[:], neg_hot).then_inc(d_nhot, 16)
            act.dma_start(wp[:], w_proj).then_inc(d_wp, 16)
            act.dma_start(wpq[:], w_proj_q).then_inc(d_wpq, 16)

            def group_rstd(b):
                act.wait_ge(gn_var[b], 1)
                act.activation(glog[:], gvar[:], ACT.Ln).then_inc(gn_log[b], 1)
                act.wait_ge(gn_log[b], 1)
                act.activation(grstd[:], glog[:], ACT.Exp, scale=-0.5).then_inc(gn_rstd[b], 1)

            def tile_stats(t):
                r, n = ROWS[t], n_cen[t]
                act.wait_ge(centred, n)
                act.activation(sq[0:r, t, :], cen_ps[t][0:r], ACT.Square).then_inc(squared, 1)

            def tile_rstd(t):
                r, n = ROWS[t], n_cen[t]
                act.wait_ge(varied, n)
                act.activation(lnl[0:r, t, :], var_ps[t][0:r], ACT.Ln, bias=vec[0:r, MASK + 1:MASK + 2]).then_inc(logged, 1)
                act.wait_ge(logged, n)
                act.activation(rstd[0:r, t, :], lnl[0:r, t, :], ACT.Exp, scale=-0.5).then_inc(rstd_set, 1)

            def move(b, g, n):
                act.wait_ge(picked[b], 4 * g + n + 1)
                act.activation((qs if n == 0 else ks)[64:128, 4 * g:4 * g + 2, :],
                               ring_bank(g, n)[64:128, :].rearrange("p (h n) -> p h n", h=2), ACT.Copy).then_inc(moved_a[b], 1)

            def rel_high(b, g, r):
                act.wait_ge(rel_done[b], 2 * g + r + 1)
                act.activation(unit_rel_dst(g, r), unit_rel_src(g, r), ACT.Copy).then_inc(rel_h[b], 1)

            def copy_maxima(b, g):
                act.wait_ge(max_t[b], g + 1)
                if b == 0 and g == 0:
                    act.wait_ge(mt_zeroed, 1)
                act.activation(mt[0:4, g, :], mt_ps, ACT.Copy).then_inc(max_c[b], 1)

            def exponentials(b, h):
                act.wait_ge(keyed[b], h + 1)
                act.activation(pt[:, h, :, :], key_banks[h % 2][:, :].rearrange("p (k n) -> p k n", k=QT),
                               ACT.Exp).then_inc(exped[b], 1)

            def group_tail(b, g):
                act.wait_ge(summed[b], g + 1)
                act.activation(slog[:, g, :], sum_ps, ACT.Ln).then_inc(s_logged[b], 1)
                act.wait_ge(s_logged[b], g + 1)
                act.activation(srec[:, g, :], slog[:, g, :], ACT.Exp, scale=-1.0).then_inc(s_rec[b], 1)

            def stage(b, s, between={}):
                g = s - 1
                if s < HG:
                    move(b, s, 0)
                if g >= 1:
                    group_tail(b, g - 1)
                if 0 in between:
                    between[0]()
                if g >= 0:
                    copy_maxima(b, g)
                if s < HG:
                    move(b, s, 2)
                    rel_high(b, s, 0)
                if 1 in between:
                    between[1]()
                if g >= 0:
                    exponentials(b, 4 * g)
                    exponentials(b, 4 * g + 1)
                if s < HG:
                    rel_high(b, s, 1)
                if 2 in between:
                    between[2]()
                if g >= 0:
                    exponentials(b, 4 * g + 2)
                    exponentials(b, 4 * g + 3)
                if 3 in between:
                    between[3]()

            def copy_lora():
                act.wait_ge(lora_t, 1)
                act.activation(lo_t[:], bank[5][0:16, 0:2 * DIM].rearrange("p (k n) -> p k n", k=2), ACT.Copy).then_inc(lora_c, 1)

            def set_picks():
                act.wait_ge(zeroed, 2)
                act.wait_ge(d_cst, 16)
                idv = ident.rearrange("p (i c) -> p i c", i=8)
                for v, blocks, scale in ((0, (0, 1), 1.0), (1, (2, 3), 1.0), (2, (0, 2), HD ** -0.5), (3, (1, 3), HD ** -0.5)):
                    for k in blocks:
                        act.activation(pick[:, v, :, 64 + 16 * k:80 + 16 * k], idv, ACT.Copy, scale=scale).then_inc(picks_set, 1)

            group_rstd(0)
            act.wait_ge(zeroed, 1)
            def pad_tile(i):
                t = order0[i]
                r = ROWS[t]
                act.wait_ge(projected[0], i + 1)
                act.wait_ge(d_vec, 16)
                act.activation(pad[0:r, t, 1:1 + SIDE, 1:1 + SIDE],
                               qkv_ps[i][0:r].rearrange("p (a c) -> p a c", a=SIDE), ACT.Identity,
                               bias=vec[0:r, BQKV0 + t:BQKV0 + t + 1]).then_inc(padded, 1)

            for i in range(3):
                pad_tile(i)
            copy_lora()
            set_picks()
            tile_stats(A)
            pad_tile(3)
            def high(t):
                act.wait_ge(full_set, n_cen[t])
                act.activation(hi[:, place3[t], :], full[:, t, :], ACT.Copy).then_inc(hi_set[0], 1)

            pad_tile(4)
            tile_stats(B)
            tile_rstd(A)
            tile_rstd(B)
            high(A)
            high(B)
            def stats_e():
                tile_stats(E)
                tile_rstd(E)

            stage(0, 0, {1: lambda: tile_stats(C), 2: lambda: tile_rstd(C), 3: stats_e})
            stage(0, 1, {0: lambda: tile_stats(D), 1: lambda: tile_rstd(D), 3: lambda: high(D)})
            stage(0, 2)
            stage(0, 3)
            group_tail(0, HG - 1)

            group_rstd(1)

            def high1(t):
                i = order1.index(t)
                act.wait_ge(projected[1], i + 1)
                act.activation(hi[:, place3[t], :], qkv1_ps[i], ACT.Identity,
                               bias=vec[:, BQKV1 + place3[t]:BQKV1 + place3[t] + 1]).then_inc(hi_set[1], 1)

            high1(A)
            high1(B)
            stage(1, 0, {1: lambda: high1(D)})
            for s in range(1, HG + 1):
                stage(1, s)
            group_tail(1, HG - 1)

        @block.vector
        def _(dve):
            def group_norm_in(b):
                if b == 0:
                    dve.wait_ge(d_x, 16)
                for t in range(2):
                    if b == 1:
                        dve.wait_ge(x_set[0], t + 1)
                    dve.bn_stats(stats[:, t, :], xs[b][:, t, :]).then_inc(gn_stat[b], 1)
                for t in range(2):
                    dve.wait_ge(gn_stat[b], t + 1)
                    dve.bn_aggr(mom[:, t, :], stats[:, t, :]).then_inc(gn_mom[b], 1)
                dve.wait_ge(gn_mom[b], 2)
                dve.tensor_copy(sums[:, 0, :], mom[:, :, 0]).then_inc(gn_sq[b], 1)
                dve.tensor_tensor(sums[:, 1, :], mom[:, :, 0], mom[:, :, 0], ALU.mult).then_inc(gn_sq[b], 1)
                dve.wait_ge(gn_sq[b], 2)
                dve.tensor_tensor(sums[:, 1, :], sums[:, 1, :], mom[:, :, 1], ALU.add).then_inc(gn_in[b], 1)

            def group_norm_out(b):
                dve.wait_ge(gn_sum[b], 1)
                dve.tensor_copy(gmean[:], misc_ps[0:HALF, 0:4].rearrange("p (k t) -> p k t", k=2)).then_inc(gn_mean[b], 1)
                dve.wait_ge(gn_mean[b], 1)
                dve.tensor_tensor(gvar[:], gmean[:, 0, :], gmean[:, 0, :], ALU.mult).then_inc(gn_msq[b], 1)
                dve.wait_ge(gn_msq[b], 1)
                dve.scalar_tensor_tensor(out=gvar[:], in0=gmean[:, 1, :], scalar=EPS, in1=gvar[:],
                                         op0=ALU.add, op1=ALU.subtract).then_inc(gn_var[b], 1)
                dve.wait_ge(gn_rstd[b], 1)
                for t in range(2):
                    dve.tensor_scalar(xn[:, t, :], xs[b][:, t, :], gmean[:, 0, t:t + 1], grstd[:, t:t + 1],
                                      ALU.subtract, ALU.mult).then_inc(xn_set[b], 1)

            def normalise(t):
                r, n = ROWS[t], n_cen[t]
                dve.wait_ge(rstd_set, n)
                dve.tensor_tensor(nrm[0:r, t, :], cen_ps[t][0:r], rstd[0:r, t, :], ALU.mult).then_inc(scaled, 1)
                dve.wait_ge(scaled, n)
                dve.tensor_scalar(full[0:r, t, :], nrm[0:r, t, :], vec[0:r, LNG0 + t:LNG0 + t + 1],
                                  vec[0:r, LNB0 + t:LNB0 + t + 1], ALU.mult, ALU.add).then_inc(full_set, 1)

            def move(b, g, n):
                dve.wait_ge(picked[b], 4 * g + n + 1)
                dve.tensor_copy((qs if n == 1 else ks)[64:128, 4 * g + 2:4 * g + 4, :],
                                ring_bank(g, n)[64:128, :].rearrange("p (h n) -> p h n", h=2)).then_inc(moved_d[b], 1)

            def rel_low(b, g, r):
                dst = unit_rel_dst(g, r)
                dve.wait_ge(rel_h[b], 2 * g + r + 1)
                dve.scalar_tensor_tensor(out=dst, in0=dst.bitcast(F32), scalar=vec[0:64, MASK:MASK + 1],
                                         in1=unit_rel_src(g, r), op0=ALU.mult, op1=ALU.add).then_inc(rel_l[b], 1)

            def maximum(b, h):
                dve.wait_ge(scored[b], h + 1)
                dve.tensor_reduce(mx[:, h, :], ring_bank(h // 4, 6 + h % 4)[:, :].rearrange("p (q n) -> p q n", q=QT),
                                  AXX, ALU.max).then_inc(maxed[b], 1)

            def o_copy(b, g):
                dve.wait_ge(weighed[b], g + 1)
                dve.tensor_copy(os_[:, g, :], o_ps).then_inc(o_copied[b], 1)

            def o_norm(b, g):
                dve.wait_ge(s_rec[b], g + 1)
                if g == HG - 1:
                    dve.wait_ge(weighed[b], g + 1)
                dve.tensor_tensor(on[:, g, :], o_ps if g == HG - 1 else os_[:, g, :], srec[:, g, :],
                                  ALU.mult).then_inc(normed[b], 1)

            def stage(b, s, between={}):
                g = s - 1
                if s < HG:
                    move(b, s, 1)
                    if 0 in between:
                        between[0]()
                    move(b, s, 3)
                    if 1 in between:
                        between[1]()
                    rel_low(b, s, 0)
                if g >= 1:
                    o_norm(b, g - 1)
                if s < HG:
                    if 2 in between:
                        between[2]()
                    rel_low(b, s, 1)
                    if 3 in between:
                        between[3]()
                    maximum(b, 4 * s)
                    maximum(b, 4 * s + 1)
                    maximum(b, 4 * s + 2)
                    if 4 in between:
                        between[4]()
                if 0 <= g < HG - 1:
                    o_copy(b, g)
                if s < HG:
                    maximum(b, 4 * s + 3)

            def add_residual(b):
                dve.wait_ge(y_done[b], 1)
                for t in range(2):
                    dve.scalar_tensor_tensor(out=xs[b + 1][:, t, :], in0=y_ps[0:HALF, t * TOK:(t + 1) * TOK],
                                             scalar=vec[0:HALF, BPROJ + 2 * b + t:BPROJ + 2 * b + t + 1],
                                             in1=xs[b][:, t, :], op0=ALU.add, op1=ALU.add).then_inc(x_set[b], 1)

            group_norm_in(0)
            group_norm_out(0)
            dve.wait_ge(d_cst, 16)
            dve.wait_ge(d_vec, 16)
            def tap_matrices(v, first, last):
                for k in range(first, last):
                    w = vec[:, TAP0 + 9 * (A, C)[v] + k:TAP0 + 9 * (A, C)[v] + k + 1]
                    dve.tensor_scalar(taps_m[:, v, k, :], centre, w, None,
                                      ALU.mult).then_inc(vtaps_set if v else qtaps_set, 1)

            tap_matrices(0, 0, TAPS)
            dve.wait_ge(d_rel, 16)
            dve.tensor_copy(relt_hi[64:128], relt[64:128]).then_inc(rel_hi, 1)
            dve.wait_ge(rel_hi, 1)
            dve.scalar_tensor_tensor(out=relt_s[64:128].rearrange("p a b -> p (a b)"),
                                     in0=relt_hi[64:128].bitcast(F32).rearrange("p a b -> p (a b)"),
                                     scalar=vec[64:128, MASK:MASK + 1],
                                     in1=relt[64:128].rearrange("p a b -> p (a b)"),
                                     op0=ALU.mult, op1=ALU.add).then_inc(rel_split, 1)
            def taps(t, first, last):
                s = (B, D).index(t)
                dst = conv[:, s, :].rearrange("p (a c) -> p a c", a=SIDE)
                for k in range(first, last):
                    src = pad[:, t, k // 3:k // 3 + SIDE, k % 3:k % 3 + SIDE]
                    w = vec[:, TAP0 + 9 * t + k:TAP0 + 9 * t + k + 1]
                    if k == 0:
                        dve.wait_ge(padded, n_padded[t])
                        dve.tensor_scalar(dst, src, w, None, ALU.mult).then_inc(conv_step[s], 1)
                    else:
                        dve.wait_ge(conv_step[s], k)
                        dve.scalar_tensor_tensor(out=dst, in0=src, scalar=w, in1=dst, op0=ALU.mult,
                                                 op1=ALU.add).then_inc(conv_step[s], 1)

            def low(t):
                i = place3[t]
                dve.wait_ge(hi_set[0], i + 1)
                dve.tensor_tensor(lo[:, i, :], full[:, t, :], hi[:, i, :].bitcast(F32), ALU.subtract).then_inc(lo_set[0], 1)

            for k in range(TAPS):
                taps(B, k, k + 1)
                tap_matrices(1, k, k + 1)
            dve.wait_ge(d_nhot, 16)
            dve.tensor_copy(ident_r[:], ident).then_inc(id_set, 1)
            dve.tensor_copy(nhot_r[:], nhot[:].rearrange("p (j n) -> p j n", j=4)).then_inc(id_set, 1)
            taps(D, 0, 4)
            normalise(A)
            low(A)
            normalise(B)
            low(B)
            taps(D, 4, 7)

            def v_to_tokens(part, h0, h1):
                dve.wait_ge(ones_set, 1)
                dve.wait_ge(v_turned, part)
                dve.tensor_copy(va[:, :, h0:h1, 0:HD],
                                turn_ps[:, 0:QT * HD * (h1 - h0)].rearrange("p (q h c) -> p q h c", q=QT, c=HD)).then_inc(v_set[0], 1)

            def add_lora():
                dve.wait_ge(d_w1, 16)
                dve.wait_ge(lora_w, 1)
                for n, col in ((0, 0), (1, 2 * DIM)):
                    for_w = w1[:, :, col:col + DIM]
                    dve.tensor_tensor(for_w, lora_ps[n], for_w, ALU.add).then_inc(w1_set, 1)

            def turned_e():
                v_to_tokens(2, 8, 12)
                normalise(D)

            stage(0, 0, {0: lambda: taps(D, 7, TAPS), 1: add_lora, 2: lambda: normalise(C)})
            normalise(E)
            stage(0, 1, {2: lambda: v_to_tokens(1, 0, 8), 3: turned_e, 4: lambda: low(D)})
            stage(0, 2)
            stage(0, 3)
            o_norm(0, HG - 1)
            add_residual(0)

            group_norm_in(1)
            group_norm_out(1)

            def low1(t):
                i = order1.index(t)
                dve.wait_ge(hi_set[1], i + 1)
                dve.scalar_tensor_tensor(out=lo[:, place3[t], :], in0=qkv1_ps[i],
                                         scalar=vec[:, BQKV1 + place3[t]:BQKV1 + place3[t] + 1],
                                         in1=hi[:, place3[t], :].bitcast(F32), op0=ALU.add, op1=ALU.subtract).then_inc(lo_set[1], 1)

            def v_in():
                dve.wait_ge(d_vb, 16)
                dve.wait_ge(v_proj, 1)
                for q in range(QT):
                    dve.tensor_tensor(va[:, q, :, 0:HD],
                                      bank[7][:, q * DIM:(q + 1) * DIM].rearrange("p (h c) -> p h c", h=HEADS),
                                      vb1[:].rearrange("p (h c) -> p h c", h=HEADS), ALU.add).then_inc(v_set[1], 1)

            low1(A)
            low1(B)
            stage(1, 0, {2: lambda: low1(D), 3: v_in})
            for s in range(1, HG + 1):
                stage(1, s)
            o_norm(1, HG - 1)
            add_residual(1)

        @block.tensor
        def _(pe):
            def warm_up(n, to=bank[6]):
                for _ in range(n):
                    pe.matmul(to[:, :], warm[:, 0:128], warm[:, :], start=True, stop=True)

            def group_sums(b):
                pe.wait_ge(gn_in[b], 1)
                pe.wait_ge(gn_sq[b], 2)
                if b == 0:
                    pe.wait_ge(d_vec, 16)
                pe.matmul(misc_ps[0:HALF, 0:4], group_avg, sums[:].rearrange("p k t -> p (k t)"),
                          start=True, stop=True).then_inc(gn_sum[b], 1)

            def project(b, i, t, w):
                for n, (p, col, width) in enumerate(PARTS[t]):
                    for k in range(2):
                        mm = pe.matmul((qkv_ps if b == 0 else qkv1_ps)[i][p:p + width, :], w[:, k, col:col + width], xn[:, k, :],
                                       start=(k == 0), stop=(k == 1))
                mm.then_inc(projected[b], 1)

            def convolve(t, v, first, last):
                r = ROWS[t]
                if first == 0:
                    pe.wait_ge(qtaps_set if v == 0 else vtaps_set, TAPS)
                    pe.wait_ge(padded, order0.index(t) + 1)
                for k in range(first, last):
                    mm = pe.matmul(cen_ps[t][0:r, :], taps_m[:, v, k, 0:r],
                                   pad[:, t, k // 3:k // 3 + SIDE, k % 3:k % 3 + SIDE],
                                   start=(k == 0), stop=(k == TAPS - 1))
                    if k == TAPS - 1:
                        mm.then_inc(centred, 1)

            def variance(t):
                r = ROWS[t]
                pe.wait_ge(squared, n_cen[t])
                if t == C:
                    pe.wait_ge(w1_set, 2)
                if t == D:
                    pe.wait_ge(logged, n_cen[E])
                pe.matmul(var_ps[t][0:r, :], average[0:r, 0:r], sq[0:r, t, :], start=True, stop=True).then_inc(varied, 1)

            def centre_tile(t):
                s = (B, D).index(t)
                pe.wait_ge(conv_step[s], TAPS)
                if t == B:
                    pe.wait_ge(lora_c, 1)
                else:
                    pe.wait_ge(w1_set, 2)
                pe.matmul(cen_ps[t], centre, conv[:, s, :], start=True, stop=True).then_inc(centred, 1)

            def turn(t):
                r = ROWS[t]
                pe.wait_ge(full_set, n_cen[t])
                if t == C:
                    pe.wait_ge(logged, n_cen[D])
                else:
                    pe.wait_ge(v_set[0], 1)
                for q in range(QT):
                    mm = pe.transpose(turn_ps[:, q * r:(q + 1) * r], full[0:r, t, q * 128:(q + 1) * 128],
                                      ident[0:r, 0:r])
                mm.then_inc(v_turned, 1)

            def ring_free(b, g, n):
                if n < 3:
                    g, n = g - 1, n + 7
                else:
                    n -= 3
                if g < 0:
                    return
                if n in (0, 2):
                    pe.wait_ge(moved_a[b], 2 * g + n // 2 + 1)
                elif n in (1, 3):
                    pe.wait_ge(moved_d[b], 2 * g + n // 2 + 1)
                elif n in (4, 5):
                    pe.wait_ge(rel_l[b], 2 * g + n - 3)
                else:
                    pe.wait_ge(maxed[b], 4 * g + n - 5)

            def pick_unit(b, g, n):
                place, v = ((q_place, 0), (k_place, 2))[n // 2]
                if g in (0, 2) and n % 2 == 0:
                    pe.wait_ge(lo_set[b], 3 if g == 2 else n // 2 + 1)
                    pe.wait_ge(picks_set, 8)
                ring_free(b, g, n)
                for j in range(2):
                    t, i = place(4 * g + 2 * (n % 2) + j)
                    dst = ring_bank(g, n)[:, j * TOK:(j + 1) * TOK]
                    pe.matmul(dst, pick[:, v, i, :], hi[:, place3[t], :], start=True, stop=False)
                    mm = pe.matmul(dst, pick[:, v + 1, i, :], lo[:, place3[t], :], start=False, stop=True)
                mm.then_inc(picked[b], 1)

            def rel_unit(b, g, r):
                if r == 0:
                    pe.wait_ge(moved_a[b], 2 * g + 1)
                    pe.wait_ge(moved_d[b], 2 * g + 1)
                    if g == 0:
                        pe.wait_ge(rel_set, 4 * b + 4)
                ring_free(b, g, 4 + r)
                heads = qs[64:128, 4 * g:4 * g + 4, :].rearrange("p h (y x) -> p x y h", x=SIDE)
                out = ring_bank(g, 4 + r)[0:64, :]
                by_x = out.rearrange("p (y x h) -> p x y h", y=8, x=SIDE)
                for x in range(SIDE):
                    pe.matmul(by_x[:, x], rel_w[64:128, 2 * b + 1, SIDE - 1 - x, 0:64], heads[:, x, 8 * r:8 * r + 8, :],
                              start=True, stop=False, skip_group_check=True)
                for i in range(8):
                    y = 8 * r + i
                    mm = pe.matmul(out[0:32, 64 * i:64 * i + 64], rel_w[64:128, 2 * b, SIDE - 1 - y, 0:32],
                                   heads[:, :, y, :], start=False, stop=True, skip_group_check=True)
                mm.then_inc(rel_done[b], 1)

            def score(b, h):
                g, n = h // 4, 6 + h % 4
                if h % 4 == 0:
                    pe.wait_ge(rel_l[b], 2 * g + 2)
                    pe.wait_ge(moved_a[b], 2 * g + 2)
                    pe.wait_ge(moved_d[b], 2 * g + 2)
                    pe.wait_ge(d_hot, 16)
                ring_free(b, g, n)
                for q in range(QT):
                    mm = pe.matmul(ring_bank(g, n)[:, q * TOK:(q + 1) * TOK], qs[:, h, q * 128:(q + 1) * 128], ks[:, h, :],
                                   start=True, stop=True)
                mm.then_inc(scored[b], 1)

            def turn_maxima(b, g):
                pe.wait_ge(maxed[b], 4 * g + 4)
                if b == 0 and g == 0:
                    pe.wait_ge(full_set, n_cen[E])
                    pe.wait_ge(id_set, 2)
                if g >= 1:
                    pe.wait_ge(s_logged[b], g)
                for q in range(QT):
                    mm = pe.matmul(mt_ps[:, q * 128:(q + 1) * 128], mx[:, 4 * g:4 * g + 4, q], ident_r[:],
                                   start=True, stop=True)
                mm.then_inc(max_t[b], 1)

            def score_by_key(b, h):
                g, j = h // 4, h % 4
                if j == 0:
                    pe.wait_ge(max_c[b], g + 1)
                if b == 0 and h == 0:
                    pe.wait_ge(full_set, n_cen[C])
                if h >= 2:
                    pe.wait_ge(exped[b], h - 1)
                for k in range(QT):
                    dst = key_banks[h % 2][:, k * TOK:(k + 1) * TOK]
                    pe.matmul(dst, ks[:, h, k * 128:(k + 1) * 128], qs[:, h, :], start=True, stop=False)
                    mm = pe.matmul(dst, nhot_r[:, j, :], mt[:, g, :], start=False, stop=True)
                mm.then_inc(keyed[b], 1)

            def weigh(b, g):
                pe.wait_ge(exped[b], 4 * g + 4)
                pe.wait_ge(v_set[b], 2)
                if g >= 1:
                    pe.wait_ge(o_copied[b], g)
                for k in range(QT):
                    for j in range(4):
                        mm = pe.matmul(o_ps[32 * j:32 * j + 32, :], va[:, k, 4 * g + j, :], pt[:, 4 * g + j, k, :],
                                       start=(k == 0), stop=(k == QT - 1), skip_group_check=True)
                mm.then_inc(weighed[b], 1)

            def spread_sums(b, g):
                pe.wait_ge(o_copied[b], g + 1)
                pe.wait_ge(max_c[b], g + 1)
                pe.matmul(sum_ps, sum_sel, os_[:, g, :], start=True, stop=True).then_inc(summed[b], 1)

            first_y = [True, True]

            def out_project(b, g):
                pe.wait_ge(normed[b], g + 1)
                if g == 0:
                    pe.wait_ge(d_wp, 16)
                for t in range(2):
                    mm = pe.matmul(y_ps[0:HALF, t * TOK:(t + 1) * TOK], wp[:, b, g, t * HALF:(t + 1) * HALF], on[:, g, :],
                                   start=first_y[b], stop=(g == 2), skip_group_check=True)
                    first_y[b] = False
                if g == 2:
                    mm.then_inc(y_done[b], 1)

            def q_project():
                pe.wait_ge(d_wpq, 16)
                for t in range(2):
                    for k, (tile, r) in enumerate(((A, 128), (D, 64))):
                        pe.matmul(y_ps[0:HALF, t * TOK:(t + 1) * TOK], wpq[0:r, k, t * HALF:(t + 1) * HALF], full[0:r, tile, :],
                                  start=first_y[0], stop=False, skip_group_check=True)
                        first_y[0] = False

            def direct_sums(b, g):
                pe.wait_ge(exped[b], 4 * g + 4)
                pe.wait_ge(zeroed, 3)
                for k in range(QT):
                    for j in range(4):
                        mm = pe.matmul(sum_ps[32 * j:32 * j + 32, :], ones[:, :], pt[:, 4 * g + j, k, :],
                                       start=(k == 0), stop=(k == QT - 1), skip_group_check=True)
                mm.then_inc(summed[b], 1)

            def stage(b, s, between={}):
                g = s - 1
                pick_unit(b, s, 0)
                if g >= 1:
                    spread_sums(b, g - 1)
                pick_unit(b, s, 1)
                if 0 in between:
                    between[0]()
                if g >= 0:
                    turn_maxima(b, g)
                pick_unit(b, s, 2)
                pick_unit(b, s, 3)
                if 1 in between:
                    between[1]()
                rel_unit(b, s, 0)
                if 2 in between:
                    between[2]()
                if g >= 0:
                    score_by_key(b, 4 * g)
                    score_by_key(b, 4 * g + 1)
                if 3 in between:
                    between[3]()
                rel_unit(b, s, 1)
                if g >= 0:
                    score_by_key(b, 4 * g + 2)
                if g >= 1:
                    out_project(b, g - 1)
                if g >= 0:
                    score_by_key(b, 4 * g + 3)
                if 4 in between:
                    between[4]()
                score(b, 4 * s)
                score(b, 4 * s + 1)
                score(b, 4 * s + 2)
                if 5 in between:
                    between[5]()
                if g >= 0:
                    weigh(b, g)
                score(b, 4 * s + 3)

            def last_stage(b):
                g = HG - 1
                spread_sums(b, g - 1)
                warm_up(2, key_banks[0])
                turn_maxima(b, g)
                warm_up(2)
                score_by_key(b, 4 * g)
                score_by_key(b, 4 * g + 1)
                out_project(b, g - 1)
                score_by_key(b, 4 * g + 2)
                warm_up(1)
                score_by_key(b, 4 * g + 3)
                warm_up(2)
                direct_sums(b, g)
                weigh(b, g)
                warm_up(3)
                out_project(b, g)

            def lora_first():
                pe.wait_ge(d_lora, 16)
                for k in range(2):
                    mm = pe.matmul(bank[5][0:16, k * DIM:(k + 1) * DIM], lo_w[:, 2 * DIM + 16 * k:2 * DIM + 16 * k + 16],
                                   lo_w[:, 0:DIM], start=True, stop=True)
                mm.then_inc(lora_t, 1)

            def lora_second():
                pe.wait_ge(lora_c, 1)
                pe.wait_ge(padded, 5)
                for k in range(2):
                    for t in range(2):
                        mm = pe.matmul(lora_ps[k][:, t, :], lo_t[:, k, t * HALF:(t + 1) * HALF], lo_w[:, DIM:2 * DIM],
                                       start=True, stop=True)
                mm.then_inc(lora_w, 1)

            pe.wait_ge(warm_set, 1)
            warm_up(WARM0)
            group_sums(0)
            lora_first()
            warm_up(WARM1)
            pe.wait_ge(xn_set[0], 2)
            pe.wait_ge(d_w0, 32)
            for i in range(3):
                project(0, i, order0[i], w0)
            convolve(A, 0, 0, TAPS)
            project(0, 3, D, w0)
            project(0, 4, E, w0)
            centre_tile(B)
            variance(A)
            variance(B)
            lora_second()
            convolve(C, 1, 0, 4)

            def e_taps(first, last):
                if first == 0:
                    pe.wait_ge(full_set, n_cen[B])
                convolve(E, 1, first, last)

            def c_and_e():
                variance(C)
                e_taps(5, TAPS)
                centre_tile(D)

            stage(0, 0, {0: lambda: convolve(C, 1, 4, TAPS), 3: lambda: e_taps(0, 5), 4: c_and_e, 5: lambda: variance(E)})
            stage(0, 1, {0: lambda: variance(D), 2: lambda: turn(C), 4: lambda: turn(E)})
            stage(0, 2, {3: q_project})
            last_stage(0)

            warm_up(5)
            group_sums(1)
            warm_up(5)
            pe.wait_ge(xn_set[1], 2)
            pe.wait_ge(w1_set, 2)
            project(1, 0, A, w1)
            project(1, 1, B, w1)

            def project_rest():
                project(1, 2, D, w1)

            def project_v():
                for q in range(QT):
                    for k in range(2):
                        mm = pe.matmul(bank[7][:, q * DIM:(q + 1) * DIM], xn[:, k, q * 128:(q + 1) * 128],
                                       w1[:, k, 2 * DIM:3 * DIM], start=(k == 0), stop=(k == 1))
                mm.then_inc(v_proj, 1)

            stage(1, 0, {2: project_rest, 4: project_v})
            stage(1, 1)
            stage(1, 2)
            last_stage(1)


def shape_constants(np):
    cst = np.zeros((128, NCST), np.float32)
    r = np.arange(128)
    same = (r[:, None] // HD == r[None, :] // HD).astype(np.float32) / HD
    cst[:, ID0:ID0 + 128] = np.eye(128, dtype=np.float32)
    cst[:, CEN0:CEN0 + 128] = np.eye(128, dtype=np.float32) - same
    cst[:, AVG0:AVG0 + 128] = same
    c = np.arange(HALF)
    vec = np.zeros((128, NVEC), np.float32)
    vec[:HALF, GRP0:GRP0 + HALF] = (c[:, None] // GROUP == c[None, :] // GROUP) / np.float32(GROUP)
    cst[:, SUM0:SUM0 + 128] = r[:, None] == r[None, :] // 32 * 32 + HD
    t = np.arange(TOK)
    hots = np.zeros((64, TOK), np.float32)
    for k in range(SIDE):
        for b in range(2):
            hots[16 * b + k] = t // SIDE == k
            hots[32 + 16 * b + k] = t % SIDE == k
    hot = np.zeros((128, 4, 128), np.float32)
    for j in range(4):
        hot[j, j] = -1.0
    return cst, hots, hot.reshape(128, 512), vec


def kernel(**inputs):
    import numpy as np
    import concourse.bacc as bacc
    from concourse.bass_utils import run_bass_kernel_spmd

    a = {k: np.asarray(v) for k, v in inputs.items()}
    cst, hots, hot, vec = shape_constants(np)
    kind = {A: "q", B: "k", C: "v", E: "v"}
    for t, parts in PARTS.items():
        for n, (p, col, width) in enumerate(parts):
            name = "qk"[n] if t == D else kind[t]
            rep = width // HD
            taps = a[f"L0_conv_w_pool_{name}"].reshape(TAPS, HD)
            vec[p:p + width, TAP0 + 9 * t:TAP0 + 9 * t + TAPS] = np.tile(taps.T, (rep, 1))
            vec[p:p + width, BQKV0 + t] = a["L0_conv_b_qkv"][col:col + width]
            vec[p:p + width, LNG0 + t] = np.tile(a[f"L0_conv_g_{name}"], rep)
            vec[p:p + width, LNB0 + t] = np.tile(a[f"L0_conv_b_{name}"], rep)
            if t in (A, B, D):
                vec[p:p + width, BQKV1 + {A: 0, B: 1, D: 2}[t]] = a["L1_conv_qkv_b"][col:col + width]
    for b, name in enumerate(("L0_conv_b_proj", "L1_conv_proj_b")):
        vec[:HALF, BPROJ + 2 * b:BPROJ + 2 * b + 2] = a[name].reshape(2, HALF).T
    vec[:, MASK] = -(np.arange(128) // HD % 2)
    vec[:, MASK + 1] = EPS

    rel = np.zeros((64, 4, REL), np.float32)
    for k, name in enumerate(("L0_conv_rel_pos_h", "L0_conv_rel_pos_w", "L1_conv_rel_pos_h", "L1_conv_rel_pos_w")):
        rel[:, k] = np.tile(a[name][REL - 1::-1].T, (4, 1))
    lora = np.concatenate([a["L1_conv_FacTu_w"].T, a["L1_conv_FacTv_w"], a["L1_conv_q_facts_w"], a["L1_conv_v_facts_w"]], 1)
    w_proj = np.zeros((HG, 4, 32, 2, DIM), np.float32)
    w_t = a["L0_conv_w_proj"].T
    w_proj[:, :, :HD, 0] = w_t.reshape(HG, 4, HD, DIM)
    w_proj[:, :, :HD, 1] = a["L1_conv_proj_w"].reshape(HG, 4, HD, DIM)
    w_proj = w_proj.reshape(HG, 128, 2, DIM).transpose(1, 2, 0, 3)
    w_proj_q = np.zeros((128, 2, DIM), np.float32)
    w_proj_q[:, 0] = w_t[:128]
    w_proj_q[:64, 1] = w_t[128:]
    arrays = {
        "x_t": a["x"].reshape(TOK, DIM).T, "w_qkv0": a["L0_conv_w_qkv"].T, "w_qkv1": a["L1_conv_qkv_w"],
        "consts": cst, "hots": hots, "vectors": vec, "neg_hot": hot, "rel": rel, "lora": lora,
        "v_bias1": np.broadcast_to(a["L1_conv_qkv_b"][2 * DIM:], (128, DIM)),
        "w_proj": w_proj, "w_proj_q": w_proj_q,
    }
    arrays = {k: np.ascontiguousarray(v) for k, v in arrays.items()}
    nc = bacc.Bacc("TRN2", target_bir_lowering=False, num_devices=1)
    args = [nc.dram_tensor(k, v.shape, F32, kind="ExternalInput").ap() for k, v in arrays.items()]
    out = nc.dram_tensor("out_t", (DIM, TOK), F32, kind="ExternalOutput").ap()
    attention_blocks(nc, *args, out)
    r = run_bass_kernel_spmd(nc, [arrays], core_ids=[0])
    y = r.results[0]["out_t"]
    return np.ascontiguousarray(y.T).reshape(1, SIDE, SIDE, DIM)
```

```python
from contextlib import ExitStack

import concourse.bass as bass
from concourse import mybir

F32 = mybir.dt.float32
F32R = mybir.dt.float32r
ALU = mybir.AluOpType
ACT = mybir.ActivationFunctionType
AXX = mybir.AxisListType.X

SIDE = 16
TOK = SIDE * SIDE
DIM = 192
HEADS = 12
HD = DIM // HEADS
HALF = DIM // 2
GROUP = 6
QT = TOK // 128
HG = HEADS // 4
REL = 2 * SIDE - 1
PADDED = SIDE + 2
TAPS = 9
EPS = 1e-5
D_SPLIT = 5

A, B, D, C, E = range(5)
PARTS = {
    A: [(0, 0, 128)],
    B: [(0, DIM, 128)],
    D: [(0, 128, 64), (64, DIM + 128, 64)],
    C: [(0, 2 * DIM, 128)],
    E: [(0, 2 * DIM + 128, 64)],
}
ROWS = {A: 128, B: 128, D: 128, C: 128, E: 64}

ID0, CEN0, AVG0, SUM0 = 0, 128, 256, 384
NCST = SUM0 + 128
TAP0 = 0
BQKV0, LNG0, LNB0 = 45, 50, 55
BQKV1 = 60
MASK = 63
GRP0 = 65
NVEC = GRP0 + HALF


def q_place(h):
    return (A, h) if h < 8 else (D, h - 8)


def k_place(h):
    return (B, h) if h < 8 else (D, h - 4)


def attention_blocks(nc, x_t, w_qkv0, w_qkv1, consts, hots, vectors, neg_hot, rel, lora, v_bias1, w_proj, w_proj_q, out_t):
    with ExitStack() as ctx:
        def sb(name, shape, dt=F32):
            return ctx.enter_context(nc.sbuf_tensor(name, shape, dt))

        def sem(name):
            return ctx.enter_context(nc.semaphore(name))

        def sems(name):
            return [sem(f"{name}_{b}") for b in range(2)]

        xs = [sb(f"x_{i}", [HALF, 2, TOK]) for i in range(3)]
        xn = sb("xn", [HALF, 2, TOK])
        stats = sb("stats", [HALF, 2, 6])
        mom = sb("mom", [HALF, 2, 2])
        sums = sb("sums", [HALF, 2])
        gmean = sb("gmean", [HALF, 2])
        gvar = sb("gvar", [HALF, 2])
        glog = sb("glog", [HALF, 2])
        grstd = sb("grstd", [HALF, 2])
        w0 = sb("w0", [HALF, 2, 3 * DIM])
        w1 = sb("w1", [HALF, 2, 3 * DIM])
        cst = sb("cst", [128, NCST])
        vec = sb("vec", [128, NVEC])
        nhot = sb("nhot", [128, 4 * 128])
        nhot_r = sb("nhot_r", [128, 4, 128], F32R)
        ident_r = sb("ident_r", [128, 128], F32R)
        relt = sb("relt", [128, 4, REL])
        relt_hi = sb("relt_hi", [128, 4, REL], F32R)
        relt_s = sb("relt_s", [128, 4, REL])
        rel_w = sb("rel_w", [128, 4, SIDE, 64], F32R)
        lo_w = sb("lo_w", [16, 4 * DIM + 32])
        lo_t = sb("lo_t", [16, 2, DIM])
        vb1 = sb("vb1", [128, DIM])
        b_row = lo_w[:, 2 * DIM + 32:].rearrange("p (b n) -> p b n", b=2)
        wp = sb("wp", [128, 2, HG, DIM])
        wpq = sb("wpq", [128, 2, DIM])
        taps_m = sb("taps_m", [128, 2, TAPS, 128])
        pick = sb("pick", [128, 4, 8, 64], F32R)
        warm = sb("warm", [128, 512], mybir.dt.bfloat16)
        pad = sb("pad", [128, 5, PADDED, PADDED])
        conv = sb("conv", [128, 2, TOK])
        conv_p = sb("conv_p", [128, 2, TOK])
        tap_p = sb("tap_p", [128, 2, TOK])
        cen_e = sb("cen_e", [64, TOK])
        sq = sb("sq", [128, 5, TOK])
        lnl = sb("lnl", [128, 5, TOK])
        rstd = sb("rstd", [128, 5, TOK])
        nrm = sb("nrm", [128, 5, TOK])
        full = sb("full", [128, 5, TOK])
        hi = sb("hi", [128, 3, TOK], F32R)
        lo = sb("lo", [128, 3, TOK], F32R)
        qs = sb("qs", [128, HEADS, TOK], F32R)
        ks = sb("ks", [128, HEADS, TOK], F32R)
        mx = sb("mx", [128, HEADS, QT], F32R)
        mt = sb("mt", [128, HG, TOK], F32R)
        pt = sb("pt", [128, HEADS, QT, TOK])
        ones = sb("ones", [128, TOK])
        va = sb("va", [128, QT, HEADS, 32])
        os_ = sb("os_", [128, HG, TOK])
        slog = sb("slog", [128, HG, TOK])
        srec = sb("srec", [128, HG, TOK])
        on = sb("on", [128, HG, TOK])

        bank = [ctx.enter_context(nc.psum_tensor(f"bank{i}", [128, 512], F32)) for i in range(8)]

        ring = [bank[0], bank[1], bank[6], bank[4]]
        key_banks = bank[2:4]
        mt_ps = bank[2][0:4, 0:TOK]
        y_ps = [bank[7][0:HALF, 0:TOK], bank[6][0:HALF, 0:TOK]]
        o_ps = [bank[5][:, 0:TOK], bank[5][:, 0:TOK], bank[1][:, 0:TOK]]
        sum_ps = [bank[5][:, 0:TOK], bank[5][:, 0:TOK], bank[0][:, 0:TOK]]
        qkv_ps = [bank[i][:, 0:TOK] for i in range(5)]
        qkv1_ps = [bank[i][:, 0:TOK] for i in (0, 3, 5)]
        cen_ps = {t: bank[i][:, 0:TOK] for t, i in ((A, 0), (B, 5), (C, 2), (D, 7), (E, 5))}
        var_ps = {t: bank[i][:, 0:TOK] for t, i in ((A, 1), (B, 6), (C, 3), (D, 3), (E, 5))}
        turn_ps, group_ps, v_ps = bank[5], bank[4][0:HALF], bank[7]

        ident = cst[:, ID0:ID0 + 128]
        centre = cst[:, CEN0:CEN0 + 128]
        average = cst[:, AVG0:AVG0 + 128]
        group_avg = vec[0:HALF, GRP0:GRP0 + HALF]
        sum_sel = cst[:, SUM0:SUM0 + 128]

        d_x, d_w0, d_cst, d_vec, d_w1 = map(sem, ("d_x", "d_w0", "d_cst", "d_vec", "d_w1"))
        d_nhot, d_rel, d_lora, d_vb, d_wp, d_wpq = map(sem, ("d_nhot", "d_rel", "d_lora", "d_vb", "d_wp", "d_wpq"))
        d_hot = sem("d_hot")
        d_out = sem("d_out")
        warm_set = sem("warm_set")
        zeroed = sem("zeroed")
        mt_zeroed = sem("mt_zeroed")
        rel_zeroed = sem("rel_zeroed")
        ones_set = sem("ones_set")
        picks_set = sem("picks_set")
        qtaps_set = sem("qtaps_set")
        vtaps_set = sem("vtaps_set")
        rel_hi = sem("rel_hi")
        rel_split = sem("rel_split")
        rel_set = sem("rel_set")
        id_set = sem("id_set")
        lora_t = sem("lora_t")
        lora_c = sem("lora_c")
        lora_w = sem("lora_w")
        w1_set = sem("w1_set")
        padded = sem("padded")
        conv_step = [sem("conv_step_k"), sem("conv_step_d")]
        p_tap = sem("p_tap")
        p_sum = sem("p_sum")
        e_copied = sem("e_copied")
        centred = sem("centred")
        squared = sem("squared")
        varied = sem("varied")
        logged = sem("logged")
        rstd_set = sem("rstd_set")
        scaled = sem("scaled")
        full_set = sem("full_set")
        v_turned = sem("v_turned")
        gn_stat, gn_mom, gn_in = map(sems, ("gn_stat", "gn_mom", "gn_in"))
        gn_sum, gn_mean, gn_msq, gn_var, gn_log, gn_rstd = map(
            sems, ("gn_sum", "gn_mean", "gn_msq", "gn_var", "gn_log", "gn_rstd"))
        xn_set = sems("xn_set")
        projected = sems("projected")
        v_proj = sem("v_proj")
        hi_set, lo_set = sems("hi_set"), sems("lo_set")
        picked = sems("picked")
        moved_a, moved_d = sems("moved_a"), sems("moved_d")
        rel_done = sems("rel_done")
        rel_h, rel_l = sems("rel_h"), sems("rel_l")
        v_set = sems("v_set")
        scored = sems("scored")
        maxed = sems("maxed")
        max_t = sems("max_t")
        max_c = sems("max_c")
        keyed = sems("keyed")
        exped = sems("exped")
        weighed = sems("weighed")
        o_copied = sems("o_copied")
        summed = sems("summed")
        s_logged, s_rec = sems("s_logged"), sems("s_rec")
        normed = sems("normed")
        y_done = sems("y_done")
        x_set = sem("x_set")
        out_ready = sems("out_ready")

        order0 = [A, B, C, D, E]
        order1 = [A, B, D]
        cen_order = [A, B, C, D, E]
        n_cen = {t: i + 1 for i, t in enumerate(cen_order)}

        place3 = {A: 0, B: 1, D: 2}
        n_padded = {t: i + 1 for i, t in enumerate(order0)}

        def unit_rel_dst(g, r):
            return qs[0:64, 4 * g:4 * g + 4, 128 * r:128 * r + 128]

        def late_k(b, s):
            return b == 0 and s == 0

        def ring_bank(g, n):
            return ring[n % 4]

        def unit_rel_src(g, r):
            return ring_bank(g, 2 + r)[0:64, :].rearrange("p (n h) -> p h n", h=4)

        lora_ps = bank[7][0:HALF, 0:2 * DIM].rearrange("p (t n) -> p t n", t=2)

        block = ctx.enter_context(nc.Block())

        @block.sync
        def _(sp):
            sp.dma_start(xs[0][:], x_t.rearrange("(t p) n -> p t n", p=HALF)).then_inc(d_x, 16)
            sp.dma_start(w0[:, :, 0:2 * DIM], w_qkv0.rearrange("(t p) n -> p t n", p=HALF)[:, :, 0:2 * DIM]).then_inc(d_w0, 16)
            sp.dma_start(w0[:, :, 2 * DIM:], w_qkv0.rearrange("(t p) n -> p t n", p=HALF)[:, :, 2 * DIM:]).then_inc(d_w0, 16)
            sp.dma_start(relt[64:128, :, :], rel).then_inc(d_rel, 16)
            sp.dma_start(w1[:], w_qkv1.rearrange("(t p) n -> p t n", p=HALF)).then_inc(d_w1, 16)
            sp.dma_start(vb1[:], v_bias1).then_inc(d_vb, 16)
            for t in range(2):
                sp.wait_ge(out_ready[t], 1)
                sp.dma_start(out_t[t * HALF:(t + 1) * HALF, :], xs[2][:, t, :]).then_inc(d_out, 16)
            sp.wait_ge(d_out, 32)

        @block.gpsimd
        def _(pool):
            pool.memset(warm[:], 0.0).then_inc(warm_set, 1)
            pool.memset(pad[:], 0.0).then_inc(zeroed, 1)
            pool.memset(rel_w[:, 0::2, :, 0:32].bitcast(F32), 0.0).then_inc(rel_zeroed, 1)
            hots_again = bass.AP(hots.tensor, hots.offset, [[TOK, 64], [0, HEADS], [1, TOK]])
            pool.wait_ge(d_cst, 16)
            pool.dma_start(ks[0:64], hots_again).then_inc(d_hot, 16)
            pool.memset(pick[:].bitcast(F32), 0.0).then_inc(zeroed, 1)
            pool.memset(ones[:], 1.0)
            pool.memset(va[:], 0.0).then_inc(zeroed, 1)
            pool.wait_ge(zeroed, 3)
            pool.memset(va[:, :, :, HD:HD + 1], 1.0).then_inc(ones_set, 1)
            pool.memset(mt[:].bitcast(F32), 0.0).then_inc(mt_zeroed, 1)
            pool.wait_ge(rel_split, 1)
            pool.wait_ge(mt_zeroed, 1)

            def windows(b):
                for k in (2 * b, 2 * b + 1):
                    row = relt_s[64:128, k, 0:1]
                    src = bass.AP(row.tensor, row.offset, [list(row.ap[0]), [1, SIDE], [1, SIDE]])
                    first = 32 if k % 2 == 0 else 0
                    for c in (first, first + 16):
                        pool.tensor_copy(rel_w[64:128, k, :, c:c + 16], src).then_inc(rel_set, 1)

            windows(0)

            def convolve_pool(t, s, first, taps_before, sums_before):
                r = ROWS[t]
                acc = conv_p[0:r, s, :]
                for i, k in enumerate(range(first, TAPS)):
                    src = pad[0:r, t, k // 3:k // 3 + SIDE, k % 3:k % 3 + SIDE]
                    w = vec[0:r, TAP0 + 9 * t + k:TAP0 + 9 * t + k + 1]
                    if i == 0:
                        pool.tensor_scalar(acc.rearrange("p (a c) -> p a c", a=SIDE), src, w, None, ALU.mult).then_inc(p_sum, 1)
                    else:
                        if i >= 3:
                            pool.wait_ge(p_sum, sums_before + i - 1)
                        tap = tap_p[0:r, i % 2, :]
                        pool.tensor_scalar(tap.rearrange("p (a c) -> p a c", a=SIDE), src, w, None, ALU.mult).then_inc(p_tap, 1)
                        pool.wait_ge(p_tap, taps_before + i)
                        pool.wait_ge(p_sum, sums_before + i)
                        pool.tensor_tensor(acc, acc, tap, ALU.add).then_inc(p_sum, 1)

            pool.wait_ge(rel_set, 4)
            pool.wait_ge(padded, n_padded[D])
            convolve_pool(D, 0, D_SPLIT, 0, 0)
            pool.wait_ge(padded, n_padded[E])
            pool.wait_ge(p_sum, TAPS - D_SPLIT)
            convolve_pool(E, 1, 0, TAPS - D_SPLIT - 1, TAPS - D_SPLIT)
            pool.wait_ge(p_sum, 2 * TAPS - D_SPLIT)
            windows(1)

        @block.scalar
        def _(act):
            act.preload_act_table_set("natural_log_exp_and_others")
            act.dma_start(vec[:], vectors).then_inc(d_vec, 16)
            act.dma_start(cst[:], consts).then_inc(d_cst, 16)
            act.dma_start(lo_w[:], lora).then_inc(d_lora, 16)
            act.dma_start(nhot[:], neg_hot).then_inc(d_nhot, 16)
            act.dma_start(wp[:], w_proj).then_inc(d_wp, 16)
            act.dma_start(wpq[:], w_proj_q).then_inc(d_wpq, 16)

            def group_rstd(b):
                act.wait_ge(gn_var[b], 1)
                act.activation(glog[:], gvar[:], ACT.Ln).then_inc(gn_log[b], 1)
                act.wait_ge(gn_log[b], 1)
                act.activation(grstd[:], glog[:], ACT.Exp, scale=-0.5).then_inc(gn_rstd[b], 1)

            def tile_stats(t):
                r, n = ROWS[t], n_cen[t]
                act.wait_ge(centred, n)
                act.activation(sq[0:r, t, :], cen_ps[t][0:r], ACT.Square).then_inc(squared, 1)

            def tile_rstd(t):
                r, n = ROWS[t], n_cen[t]
                act.wait_ge(varied, n)
                act.activation(lnl[0:r, t, :], var_ps[t][0:r], ACT.Ln, bias=vec[0:r, MASK + 1:MASK + 2]).then_inc(logged, 1)
                act.wait_ge(logged, n)
                act.activation(rstd[0:r, t, :], lnl[0:r, t, :], ACT.Exp, scale=-0.5).then_inc(rstd_set, 1)

            def move(b, g, n):
                act.wait_ge(picked[b], 2 * g + n + 1)
                act.activation((qs, ks)[n][64:128, 4 * g:4 * g + 4:2, :],
                               ring_bank(g, n)[0:64, :].rearrange("p (h n) -> p h n", h=2), ACT.Copy).then_inc(moved_a[b], 1)

            def rel_high(b, g, r):
                act.wait_ge(rel_done[b], 2 * g + r + 1)
                act.activation(unit_rel_dst(g, r), unit_rel_src(g, r), ACT.Copy).then_inc(rel_h[b], 1)

            def copy_maxima(b, g):
                act.wait_ge(max_t[b], g + 1)
                if b == 0 and g == 0:
                    act.wait_ge(mt_zeroed, 1)
                act.activation(mt[0:4, g, :], mt_ps, ACT.Copy).then_inc(max_c[b], 1)

            def exponentials(b, h):
                act.wait_ge(keyed[b], h + 1)
                act.activation(pt[:, h, :, :], key_banks[h % 2][:, :].rearrange("p (k n) -> p k n", k=QT),
                               ACT.Exp).then_inc(exped[b], 1)

            def o_copy(b, g):
                act.wait_ge(weighed[b], g + 1)
                act.activation(os_[:, g, :], o_ps[g], ACT.Copy).then_inc(o_copied[b], 1)

            def group_tail(b, g):
                act.wait_ge(summed[b], g + 1)
                act.activation(slog[:, g, :], sum_ps[g], ACT.Ln).then_inc(s_logged[b], 1)
                act.wait_ge(s_logged[b], g + 1)
                act.activation(srec[:, g, :], slog[:, g, :], ACT.Exp, scale=-1.0).then_inc(s_rec[b], 1)

            def stage(b, s, between={}):
                g = s - 1
                move(b, s, 0)
                if not late_k(b, s):
                    move(b, s, 1)
                if g >= 1:
                    group_tail(b, g - 1)
                if 0 in between:
                    between[0]()
                if g >= 0:
                    copy_maxima(b, g)
                rel_high(b, s, 0)
                rel_high(b, s, 1)
                if late_k(b, s):
                    move(b, s, 1)
                if 1 in between:
                    between[1]()
                if g >= 0:
                    exponentials(b, 4 * g)
                    exponentials(b, 4 * g + 1)
                if 2 in between:
                    between[2]()
                if g >= 0:
                    exponentials(b, 4 * g + 2)
                    exponentials(b, 4 * g + 3)
                if 3 in between:
                    between[3]()
                if g >= 0:
                    o_copy(b, g)

            def last_stage(b):
                copy_maxima(b, HG - 1)
                for j in range(4):
                    exponentials(b, 4 * (HG - 1) + j)
                group_tail(b, HG - 2)
                group_tail(b, HG - 1)

            def copy_lora():
                act.wait_ge(lora_t, 1)
                act.activation(lo_t[:], bank[5][0:16, 0:2 * DIM].rearrange("p (k n) -> p k n", k=2), ACT.Copy).then_inc(lora_c, 1)

            def set_picks():
                act.wait_ge(zeroed, 2)
                act.wait_ge(d_cst, 16)
                idv = ident.rearrange("p (i c) -> p i c", i=8)
                for v, blocks, scale in ((0, (0, 1), 1.0), (1, (2, 3), 1.0), (2, (0, 2), HD ** -0.5), (3, (1, 3), HD ** -0.5)):
                    for k in blocks:
                        act.activation(pick[:, v, :, 16 * k:16 * k + 16], idv, ACT.Copy, scale=scale).then_inc(picks_set, 1)

            def pad_tile(i):
                t = order0[i]
                r = ROWS[t]
                act.wait_ge(projected[0], i + 1)
                act.wait_ge(d_vec, 16)
                act.activation(pad[0:r, t, 1:1 + SIDE, 1:1 + SIDE],
                               qkv_ps[i][0:r].rearrange("p (a c) -> p a c", a=SIDE), ACT.Identity,
                               bias=vec[0:r, BQKV0 + t:BQKV0 + t + 1]).then_inc(padded, 1)

            def high(t):
                act.wait_ge(full_set, n_cen[t])
                act.activation(hi[:, place3[t], :], full[:, t, :], ACT.Copy).then_inc(hi_set[0], 1)

            def stats_e():
                tile_stats(E)
                act.activation(cen_e[:], cen_ps[E][0:64], ACT.Copy).then_inc(e_copied, 1)

            def v_to_tokens_e():
                act.wait_ge(v_turned, 2)
                act.wait_ge(ones_set, 1)
                act.activation(va[:, :, 8:12, 0:HD],
                               turn_ps[:, 0:QT * HD * 4].rearrange("p (q h c) -> p q h c", q=QT, c=HD), ACT.Copy).then_inc(v_set[0], 1)

            group_rstd(0)
            act.wait_ge(zeroed, 1)
            pad_tile(0)
            pad_tile(1)
            copy_lora()
            set_picks()
            tile_stats(A)
            pad_tile(2)
            tile_rstd(A)
            pad_tile(3)
            tile_stats(B)
            pad_tile(4)
            high(A)
            tile_rstd(B)
            stage(0, 0, {0: lambda: high(B), 1: lambda: tile_stats(C), 2: lambda: tile_rstd(C), 3: lambda: tile_stats(D)})
            stage(0, 1, {0: lambda: tile_rstd(D), 1: lambda: high(D)})
            stage(0, 2, {1: stats_e, 2: lambda: tile_rstd(E), 3: v_to_tokens_e})
            last_stage(0)

            for t in range(2):
                act.wait_ge(gn_stat[1], t + 1)
                act.activation(xs[1][:, t, :], y_ps[t], ACT.Copy).then_inc(x_set, 1)
            group_rstd(1)

            def high1(t):
                i = order1.index(t)
                act.wait_ge(projected[1], i + 1)
                act.activation(hi[:, place3[t], :], qkv1_ps[i], ACT.Identity,
                               bias=vec[:, BQKV1 + place3[t]:BQKV1 + place3[t] + 1]).then_inc(hi_set[1], 1)

            high1(A)
            high1(B)
            stage(1, 0)
            high1(D)
            stage(1, 1)
            stage(1, 2)
            last_stage(1)
            act.wait_ge(y_done[1], 2)
            act.activation(xs[2][:, 1, :], y_ps[1], ACT.Copy).then_inc(out_ready[1], 1)

        @block.vector
        def _(dve):
            def stream(b, t):
                return xs[0][:, t, :] if b == 0 else y_ps[t]

            def group_norm_in(b):
                if b == 0:
                    dve.wait_ge(d_x, 16)
                for t in range(2):
                    if b == 1:
                        dve.wait_ge(y_done[0], t + 1)
                    dve.bn_stats(stats[:, t, :], stream(b, t)).then_inc(gn_stat[b], 1)
                for t in range(2):
                    dve.wait_ge(gn_stat[b], t + 1)
                    dve.bn_aggr(mom[:, t, :], stats[:, t, :]).then_inc(gn_mom[b], 1)
                dve.wait_ge(gn_mom[b], 2)
                dve.tensor_tensor(sums[:], mom[:, :, 0], mom[:, :, 0], ALU.mult).then_inc(gn_in[b], 1)

            def group_norm_out(b):
                dve.wait_ge(gn_sum[b], 1)
                dve.tensor_copy(gmean[:], group_ps[:, 0:4:2]).then_inc(gn_mean[b], 1)
                dve.wait_ge(gn_mean[b], 1)
                dve.tensor_tensor(gvar[:], gmean[:], gmean[:], ALU.mult).then_inc(gn_msq[b], 1)
                dve.wait_ge(gn_msq[b], 1)
                dve.scalar_tensor_tensor(out=gvar[:], in0=group_ps[:, 1:4:2], scalar=EPS, in1=gvar[:],
                                         op0=ALU.add, op1=ALU.subtract).then_inc(gn_var[b], 1)
                dve.wait_ge(gn_rstd[b], 1)
                for t in range(2):
                    if b == 1:
                        dve.wait_ge(x_set, t + 1)
                    dve.tensor_scalar(xn[:, t, :], stream(b, t), gmean[:, t:t + 1], grstd[:, t:t + 1],
                                      ALU.subtract, ALU.mult).then_inc(xn_set[b], 1)

            def normalise(t):
                r, n = ROWS[t], n_cen[t]
                dve.wait_ge(rstd_set, n)
                dve.tensor_tensor(nrm[0:r, t, :], cen_e[:] if t == E else cen_ps[t][0:r], rstd[0:r, t, :], ALU.mult).then_inc(scaled, 1)
                dve.wait_ge(scaled, n)
                dve.tensor_scalar(full[0:r, t, :], nrm[0:r, t, :], vec[0:r, LNG0 + t:LNG0 + t + 1],
                                  vec[0:r, LNB0 + t:LNB0 + t + 1], ALU.mult, ALU.add).then_inc(full_set, 1)

            def move(b, g, n):
                dve.wait_ge(picked[b], 2 * g + n + 1)
                dve.tensor_copy((qs, ks)[n][64:128, 4 * g + 1:4 * g + 4:2, :],
                                ring_bank(g, n)[64:128, :].rearrange("p (h n) -> p h n", h=2)).then_inc(moved_d[b], 1)

            def rel_low(b, g, r):
                dst = unit_rel_dst(g, r)
                dve.wait_ge(rel_h[b], 2 * g + r + 1)
                dve.scalar_tensor_tensor(out=dst, in0=dst.bitcast(F32), scalar=vec[0:64, MASK:MASK + 1],
                                         in1=unit_rel_src(g, r), op0=ALU.mult, op1=ALU.add).then_inc(rel_l[b], 1)

            def maximum(b, h):
                dve.wait_ge(scored[b], h + 1)
                dve.tensor_reduce(mx[:, h, :], ring_bank(h // 4, 4 + h % 4)[:, :].rearrange("p (q n) -> p q n", q=QT),
                                  AXX, ALU.max).then_inc(maxed[b], 1)

            def o_norm(b, g):
                dve.wait_ge(s_rec[b], g + 1)
                if g == HG - 1:
                    dve.wait_ge(weighed[b], g + 1)
                dve.tensor_tensor(on[:, g, :], o_ps[g] if g == HG - 1 else os_[:, g, :], srec[:, g, :],
                                  ALU.mult).then_inc(normed[b], 1)

            def stage(b, s, between={}):
                move(b, s, 0)
                if 0 in between:
                    between[0]()
                if not late_k(b, s):
                    move(b, s, 1)
                if 1 in between:
                    between[1]()
                rel_low(b, s, 0)
                if 4 in between:
                    between[4]()
                rel_low(b, s, 1)
                if late_k(b, s):
                    move(b, s, 1)
                if s >= 2:
                    o_norm(b, s - 2)
                if 2 in between:
                    between[2]()
                maximum(b, 4 * s)
                maximum(b, 4 * s + 1)
                if 3 in between:
                    between[3]()
                maximum(b, 4 * s + 2)
                maximum(b, 4 * s + 3)

            group_norm_in(0)
            group_norm_out(0)
            dve.wait_ge(d_cst, 16)
            dve.wait_ge(d_vec, 16)

            def tap_matrices(v, first, last):
                for k in range(first, last):
                    w = vec[:, TAP0 + 9 * (A, C)[v] + k:TAP0 + 9 * (A, C)[v] + k + 1]
                    dve.tensor_scalar(taps_m[:, v, k, :], centre, w, None,
                                      ALU.mult).then_inc(vtaps_set if v else qtaps_set, 1)

            tap_matrices(0, 0, TAPS)
            dve.wait_ge(d_rel, 16)
            dve.tensor_copy(relt_hi[64:128], relt[64:128]).then_inc(rel_hi, 1)
            dve.wait_ge(rel_hi, 1)
            dve.scalar_tensor_tensor(out=relt_s[64:128].rearrange("p a b -> p (a b)"),
                                     in0=relt_hi[64:128].bitcast(F32).rearrange("p a b -> p (a b)"),
                                     scalar=vec[64:128, MASK:MASK + 1],
                                     in1=relt[64:128].rearrange("p a b -> p (a b)"),
                                     op0=ALU.mult, op1=ALU.add).then_inc(rel_split, 1)

            def taps(t, first, last):
                s = (B, D).index(t)
                dst = conv[:, s, :].rearrange("p (a c) -> p a c", a=SIDE)
                for k in range(first, last):
                    src = pad[:, t, k // 3:k // 3 + SIDE, k % 3:k % 3 + SIDE]
                    w = vec[:, TAP0 + 9 * t + k:TAP0 + 9 * t + k + 1]
                    if k == 0:
                        dve.wait_ge(padded, n_padded[t])
                        dve.tensor_scalar(dst, src, w, None, ALU.mult).then_inc(conv_step[s], 1)
                    else:
                        dve.wait_ge(conv_step[s], k)
                        dve.scalar_tensor_tensor(out=dst, in0=src, scalar=w, in1=dst, op0=ALU.mult,
                                                 op1=ALU.add).then_inc(conv_step[s], 1)

            def add_lora(k):
                dve.wait_ge(d_w1, 16)
                dve.wait_ge(lora_w, k + 1)
                for_w = w1[:, :, 2 * DIM * k:2 * DIM * k + DIM]
                dve.tensor_tensor(for_w, lora_ps, for_w, ALU.add).then_inc(w1_set, 1)

            def low(t):
                i = place3[t]
                dve.wait_ge(hi_set[0], i + 1)
                dve.tensor_tensor(lo[:, i, :], full[:, t, :], hi[:, i, :].bitcast(F32), ALU.subtract).then_inc(lo_set[0], 1)

            for k in range(TAPS):
                taps(B, k, k + 1)
                tap_matrices(1, k, k + 1)
            normalise(A)
            dve.wait_ge(d_nhot, 16)
            dve.tensor_copy(ident_r[:], ident).then_inc(id_set, 1)
            dve.tensor_copy(nhot_r[:], nhot[:].rearrange("p (j n) -> p j n", j=4)).then_inc(id_set, 1)
            low(A)
            taps(D, 0, 2)

            def k_in():
                normalise(B)
                low(B)

            def v_to_tokens():
                dve.wait_ge(ones_set, 1)
                dve.wait_ge(v_turned, 1)
                dve.tensor_copy(va[:, :, 0:8, 0:HD],
                                turn_ps[:, 0:QT * HD * 8].rearrange("p (q h c) -> p q h c", q=QT, c=HD)).then_inc(v_set[0], 1)

            def low_d_and_v():
                low(D)
                v_to_tokens()
                add_lora(0)

            stage(0, 0, {0: k_in, 2: lambda: taps(D, 2, 4), 3: lambda: taps(D, 4, D_SPLIT)})
            normalise(C)
            stage(0, 1, {1: lambda: normalise(D), 2: low_d_and_v})
            stage(0, 2, {1: lambda: add_lora(1), 2: lambda: normalise(E)})
            o_norm(0, HG - 2)
            o_norm(0, HG - 1)

            group_norm_in(1)
            group_norm_out(1)

            def low1(t):
                i = order1.index(t)
                dve.wait_ge(hi_set[1], i + 1)
                dve.scalar_tensor_tensor(out=lo[:, place3[t], :], in0=qkv1_ps[i],
                                         scalar=vec[:, BQKV1 + place3[t]:BQKV1 + place3[t] + 1],
                                         in1=hi[:, place3[t], :].bitcast(F32), op0=ALU.add, op1=ALU.subtract).then_inc(lo_set[1], 1)

            def v_in():
                dve.wait_ge(d_vb, 16)
                dve.wait_ge(v_proj, 1)
                for q in range(QT):
                    dve.tensor_tensor(va[:, q, :, 0:HD],
                                      v_ps[:, q * DIM:(q + 1) * DIM].rearrange("p (h c) -> p h c", h=HEADS),
                                      vb1[:].rearrange("p (h c) -> p h c", h=HEADS), ALU.add).then_inc(v_set[1], 1)

            low1(A)
            low1(B)
            stage(1, 0)
            low1(D)
            stage(1, 1, {1: v_in})
            stage(1, 2)
            o_norm(1, HG - 2)
            o_norm(1, HG - 1)
            dve.wait_ge(y_done[1], 1)
            dve.tensor_copy(xs[2][:, 0, :], y_ps[0]).then_inc(out_ready[0], 1)

        @block.tensor
        def _(pe):
            def warm_up(n, to=bank[6]):
                for _ in range(n):
                    pe.matmul(to[:, :], warm[:, 0:128], warm[:, :], start=True, stop=True)

            def group_sums(b):
                pe.wait_ge(gn_in[b], 1)
                if b == 0:
                    pe.wait_ge(d_vec, 16)
                pe.matmul(group_ps[:, 0:4], group_avg, mom[:].rearrange("p t k -> p (t k)"), start=True, stop=False)
                pe.matmul(group_ps[:, 1:4:2], group_avg, sums[:], start=False, stop=True).then_inc(gn_sum[b], 1)

            def project(b, i, t, w):
                for n, (p, col, width) in enumerate(PARTS[t]):
                    for k in range(2):
                        if i == 0:
                            pe.wait_ge(xn_set[b], k + 1)
                        mm = pe.matmul((qkv_ps if b == 0 else qkv1_ps)[i][p:p + width, :], w[:, k, col:col + width], xn[:, k, :],
                                       start=(k == 0), stop=(k == 1))
                mm.then_inc(projected[b], 1)

            def convolve(t, v, first, last):
                r = ROWS[t]
                if first == 0:
                    pe.wait_ge(qtaps_set if v == 0 else vtaps_set, TAPS)
                    pe.wait_ge(padded, order0.index(t) + 1)
                for k in range(first, last):
                    mm = pe.matmul(cen_ps[t][0:r, :], taps_m[:, v, k, 0:r],
                                   pad[:, t, k // 3:k // 3 + SIDE, k % 3:k % 3 + SIDE],
                                   start=(k == 0), stop=(k == TAPS - 1))
                    if k == TAPS - 1:
                        mm.then_inc(centred, 1)

            def variance(t):
                r = ROWS[t]
                pe.wait_ge(squared, n_cen[t])
                if t == D:
                    pe.wait_ge(logged, n_cen[C])
                if t == E:
                    pe.wait_ge(e_copied, 1)
                pe.matmul(var_ps[t][0:r, :], average[0:r, 0:r], sq[0:r, t, :], start=True, stop=True).then_inc(varied, 1)

            def centre_tile(t):
                r = ROWS[t]
                if t == B:
                    pe.wait_ge(conv_step[0], TAPS)
                    pe.wait_ge(lora_c, 1)
                    parts = [conv[:, 0, :]]
                elif t == D:
                    pe.wait_ge(conv_step[1], D_SPLIT)
                    pe.wait_ge(p_sum, TAPS - D_SPLIT)
                    parts = [conv[:, 1, :], conv_p[:, 0, :]]
                else:
                    pe.wait_ge(p_sum, 2 * TAPS - D_SPLIT)
                    pe.wait_ge(s_logged[0], 1)
                    parts = [conv_p[0:64, 1, :]]
                for n, part in enumerate(parts):
                    mm = pe.matmul(cen_ps[t][0:r], centre[0:r, 0:r], part, start=(n == 0), stop=(n == len(parts) - 1))
                mm.then_inc(centred, 1)

            def turn(t):
                r = ROWS[t]
                pe.wait_ge(full_set, n_cen[t])
                if t == C:
                    pe.wait_ge(full_set, n_cen[B])
                for q in range(QT):
                    mm = pe.transpose(turn_ps[:, q * r:(q + 1) * r], full[0:r, t, q * 128:(q + 1) * 128],
                                      ident[0:r, 0:r])
                mm.then_inc(v_turned, 1)

            def ring_free(b, g, n):
                if n < 4:
                    g, n = g - 1, n + 4
                else:
                    n -= 4
                if g < 0:
                    return
                if n < 2:
                    pe.wait_ge(moved_a[b], 2 * g + n + 1)
                    pe.wait_ge(moved_d[b], 2 * g + n + 1)
                elif n < 4:
                    pe.wait_ge(rel_l[b], 2 * g + n - 1)
                else:
                    pe.wait_ge(maxed[b], 4 * g + n - 3)

            def pick_unit(b, g, n):
                place, v = ((q_place, 0), (k_place, 2))[n]
                if g in (0, 2):
                    pe.wait_ge(lo_set[b], 3 if g == 2 else n + 1)
                    pe.wait_ge(picks_set, 8)
                ring_free(b, g, n)
                for j in range(2):
                    t, i = place(4 * g + 2 * j)
                    dst = ring_bank(g, n)[:, j * TOK:(j + 1) * TOK]
                    pe.matmul(dst, pick[:, v, i:i + 2, :], hi[:, place3[t], :], start=True, stop=False)
                    mm = pe.matmul(dst, pick[:, v + 1, i:i + 2, :], lo[:, place3[t], :], start=False, stop=True)
                mm.then_inc(picked[b], 1)

            def rel_unit(b, g, r):
                if r == 0:
                    pe.wait_ge(moved_a[b], 2 * g + 1)
                    pe.wait_ge(moved_d[b], 2 * g + 1)
                    if g == 0:
                        pe.wait_ge(rel_set, 4 * b + 4)
                ring_free(b, g, 2 + r)
                if b == 0 and g == 0 and r == 1:
                    pe.wait_ge(padded, 5)
                heads = qs[64:128, 4 * g:4 * g + 4, :].rearrange("p h (y x) -> p x y h", x=SIDE)
                out = ring_bank(g, 2 + r)[0:64, :]
                by_x = out[0:32].rearrange("p (y x h) -> p x y h", y=8, x=SIDE)
                for i in range(8):
                    y = 8 * r + i
                    pe.matmul(out[:, 64 * i:64 * i + 64], rel_w[64:128, 2 * b, SIDE - 1 - y, 0:64],
                              heads[:, :, y, :], start=True, stop=False, skip_group_check=True)
                for x in range(SIDE):
                    mm = pe.matmul(by_x[:, x], rel_w[64:128, 2 * b + 1, SIDE - 1 - x, 0:32], heads[:, x, 8 * r:8 * r + 8, :],
                                   start=False, stop=True, skip_group_check=True)
                mm.then_inc(rel_done[b], 1)

            def score(b, h):
                g, n = h // 4, 4 + h % 4
                if h % 4 == 0:
                    pe.wait_ge(rel_l[b], 2 * g + 2)
                    pe.wait_ge(moved_a[b], 2 * g + 2)
                    pe.wait_ge(moved_d[b], 2 * g + 2)
                    pe.wait_ge(d_hot, 16)
                ring_free(b, g, n)
                for q in range(QT):
                    mm = pe.matmul(ring_bank(g, n)[:, q * TOK:(q + 1) * TOK], qs[:, h, q * 128:(q + 1) * 128], ks[:, h, :],
                                   start=True, stop=True)
                mm.then_inc(scored[b], 1)

            def turn_maxima(b, g):
                pe.wait_ge(maxed[b], 4 * g + 4)
                if b == 0 and g == 0:
                    pe.wait_ge(full_set, n_cen[C])
                    pe.wait_ge(id_set, 2)
                if g >= 1:
                    pe.wait_ge(exped[b], 4 * g - 1)
                for q in range(QT):
                    mm = pe.matmul(mt_ps[:, q * 128:(q + 1) * 128], mx[:, 4 * g:4 * g + 4, q], ident_r[:],
                                   start=True, stop=True)
                mm.then_inc(max_t[b], 1)

            def score_by_key(b, h):
                g, j = h // 4, h % 4
                if j == 0:
                    pe.wait_ge(max_c[b], g + 1)
                if b == 0 and h == 1:
                    pe.wait_ge(logged, n_cen[D])
                if h >= 2:
                    pe.wait_ge(exped[b], h - 1)
                for k in range(QT):
                    dst = key_banks[h % 2][:, k * TOK:(k + 1) * TOK]
                    pe.matmul(dst, ks[:, h, k * 128:(k + 1) * 128], qs[:, h, :], start=True, stop=False)
                    mm = pe.matmul(dst, nhot_r[:, j, :], mt[:, g, :], start=False, stop=True)
                mm.then_inc(keyed[b], 1)

            def weigh(b, g):
                pe.wait_ge(exped[b], 4 * g + 4)
                pe.wait_ge(v_set[b], 1 if b == 0 and g == 0 else 2)
                if b == 1 and g == 0:
                    pe.wait_ge(lo_set[1], 3)
                if g == 1:
                    pe.wait_ge(s_logged[b], 1)
                for k in range(QT):
                    for j in range(4):
                        mm = pe.matmul(o_ps[g][32 * j:32 * j + 32, :], va[:, k, 4 * g + j, :], pt[:, 4 * g + j, k, :],
                                       start=(k == 0), stop=(k == QT - 1), skip_group_check=True)
                mm.then_inc(weighed[b], 1)

            def spread_sums(b, g):
                pe.wait_ge(o_copied[b], g + 1)
                pe.matmul(sum_ps[g], sum_sel, os_[:, g, :], start=True, stop=True).then_inc(summed[b], 1)

            first_y = [[True, True], [True, True]]

            def onto_y(b, t, weights, moving, stop=False):
                mm = pe.matmul(y_ps[t], weights, moving, start=first_y[b][t], stop=stop, skip_group_check=True)
                first_y[b][t] = False
                return mm

            def out_project(b, g, t):
                pe.wait_ge(normed[b], g + 1)
                pe.wait_ge(d_wp, 16)
                mm = onto_y(b, t, wp[:, b, g, t * HALF:(t + 1) * HALF], on[:, g, :], stop=(g == HG - 1))
                if g == HG - 1:
                    mm.then_inc(y_done[b], 1)

            def q_project(t):
                pe.wait_ge(d_wpq, 16)
                for k, (tile, r) in enumerate(((A, 128), (D, 64))):
                    onto_y(0, t, wpq[0:r, k, t * HALF:(t + 1) * HALF], full[0:r, tile, :])

            def direct_sums(b, g):
                pe.wait_ge(exped[b], 4 * g + 4)
                pe.wait_ge(zeroed, 3)
                for k in range(QT):
                    for j in range(4):
                        mm = pe.matmul(sum_ps[g][32 * j:32 * j + 32, :], ones[:, 0:32], pt[:, 4 * g + j, k, :],
                                       start=(k == 0), stop=(k == QT - 1), skip_group_check=True)
                mm.then_inc(summed[b], 1)

            def stage(b, s, between={}):
                g = s - 1
                pick_unit(b, s, 0)
                if 0 in between:
                    between[0]()
                if not late_k(b, s):
                    pick_unit(b, s, 1)
                if g >= 1:
                    spread_sums(b, g - 1)
                if 1 in between:
                    between[1]()
                if g >= 0:
                    turn_maxima(b, g)
                rel_unit(b, s, 0)
                if 2 in between:
                    between[2]()
                rel_unit(b, s, 1)
                if late_k(b, s):
                    pick_unit(b, s, 1)
                if g >= 0:
                    score_by_key(b, 4 * g)
                    score_by_key(b, 4 * g + 1)
                if 3 in between:
                    between[3]()
                if g >= 0:
                    score_by_key(b, 4 * g + 2)
                    score_by_key(b, 4 * g + 3)
                if 4 in between:
                    between[4]()
                score(b, 4 * s)
                score(b, 4 * s + 1)
                score(b, 4 * s + 2)
                if 5 in between:
                    between[5]()
                score(b, 4 * s + 3)
                if g >= 1:
                    out_project(b, g - 1, 0)
                if g >= 0:
                    weigh(b, g)

            def add_input(b, t):
                if b == 1:
                    pe.wait_ge(x_set, 2)
                    pe.wait_ge(v_set[1], 2)
                onto_y(b, t, ident[0:HALF, 0:HALF], xs[b][:, t, :])
                onto_y(b, t, b_row[0:1, b, t * HALF:(t + 1) * HALF], ones[0:1, :])

            def last_stage(b):
                g = HG - 1
                turn_maxima(b, g)
                spread_sums(b, g - 1)
                out_project(b, 0, 1)
                score_by_key(b, 4 * g)
                score_by_key(b, 4 * g + 1)
                add_input(b, 1)
                score_by_key(b, 4 * g + 2)
                score_by_key(b, 4 * g + 3)
                if b == 0:
                    q_project(1)
                direct_sums(b, g)
                weigh(b, g)
                out_project(b, 1, 0)
                out_project(b, 1, 1)
                out_project(b, 2, 0)
                out_project(b, 2, 1)

            def lora_first():
                pe.wait_ge(d_lora, 16)
                for k in range(2):
                    mm = pe.matmul(bank[5][0:16, k * DIM:(k + 1) * DIM], lo_w[:, 2 * DIM + 16 * k:2 * DIM + 16 * k + 16],
                                   lo_w[:, 0:DIM], start=True, stop=True)
                mm.then_inc(lora_t, 1)

            def lora_second(k):
                pe.wait_ge(lora_c, 1)
                if k == 0:
                    pe.wait_ge(full_set, n_cen[D])
                else:
                    pe.wait_ge(w1_set, 1)
                for t in range(2):
                    mm = pe.matmul(lora_ps[:, t, :], lo_t[:, k, t * HALF:(t + 1) * HALF], lo_w[:, DIM:2 * DIM],
                                   start=True, stop=True)
                mm.then_inc(lora_w, 1)

            pe.wait_ge(warm_set, 1)
            warm_up(7)
            group_sums(0)
            warm_up(4)
            lora_first()
            pe.wait_ge(d_w0, 32)
            project(0, 0, A, w0)
            project(0, 1, B, w0)
            convolve(A, 0, 0, TAPS)
            project(0, 2, C, w0)
            variance(A)
            project(0, 3, D, w0)
            centre_tile(B)
            project(0, 4, E, w0)
            variance(B)
            convolve(C, 1, 0, 2)

            def q_and_e():
                pe.wait_ge(w1_set, 2)
                centre_tile(E)
                q_project(0)

            def x_and_e():
                variance(E)
                add_input(0, 0)

            stage(0, 0, {0: lambda: convolve(C, 1, 2, 5), 4: lambda: convolve(C, 1, 5, TAPS)})
            variance(C)
            centre_tile(D)
            warm_up(1, bank[5])
            stage(0, 1, {0: lambda: variance(D), 1: lambda: warm_up(1, bank[5]), 3: lambda: turn(C), 4: lambda: lora_second(0)})
            stage(0, 2, {1: lambda: lora_second(1), 2: q_and_e, 3: x_and_e, 5: lambda: turn(E)})
            last_stage(0)

            warm_up(5, bank[2])
            group_sums(1)
            warm_up(5, bank[2])
            project(1, 0, A, w1)
            project(1, 1, B, w1)

            def project_rest():
                project(1, 2, D, w1)
                warm_up(2, bank[2])

            def project_v(q):
                for k in range(2):
                    mm = pe.matmul(v_ps[:, q * DIM:(q + 1) * DIM], xn[:, k, q * 128:(q + 1) * 128],
                                   w1[:, k, 2 * DIM:3 * DIM], start=(k == 0), stop=(k == 1))
                if q == 1:
                    mm.then_inc(v_proj, 1)

            project_v(0)
            stage(1, 0, {0: lambda: project_v(1), 4: project_rest, 5: lambda: warm_up(1, bank[2])})
            stage(1, 1, {0: lambda: warm_up(2, bank[2]), 1: lambda: warm_up(3, bank[2]), 3: lambda: add_input(1, 0)})
            stage(1, 2)
            last_stage(1)


def shape_constants(np):
    cst = np.zeros((128, NCST), np.float32)
    r = np.arange(128)
    same = (r[:, None] // HD == r[None, :] // HD).astype(np.float32) / HD
    cst[:, ID0:ID0 + 128] = np.eye(128, dtype=np.float32)
    cst[:, CEN0:CEN0 + 128] = np.eye(128, dtype=np.float32) - same
    cst[:, AVG0:AVG0 + 128] = same
    c = np.arange(HALF)
    vec = np.zeros((128, NVEC), np.float32)
    vec[:HALF, GRP0:GRP0 + HALF] = (c[:, None] // GROUP == c[None, :] // GROUP) / np.float32(GROUP)
    cst[:, SUM0:SUM0 + 128] = r[:, None] == r[None, :] // 32 * 32 + HD
    t = np.arange(TOK)
    hots = np.zeros((64, TOK), np.float32)
    for k in range(SIDE):
        for b in range(2):
            hots[16 * b + k] = t % SIDE == k
            hots[32 + 16 * b + k] = t // SIDE == k
    hot = np.zeros((128, 4, 128), np.float32)
    for j in range(4):
        hot[j, j] = -1.0
    return cst, hots, hot.reshape(128, 512), vec


def kernel(**inputs):
    import numpy as np
    import concourse.bacc as bacc
    from concourse.bass_utils import run_bass_kernel_spmd

    a = {k: np.asarray(v) for k, v in inputs.items()}
    cst, hots, hot, vec = shape_constants(np)
    kind = {A: "q", B: "k", C: "v", E: "v"}
    for t, parts in PARTS.items():
        for n, (p, col, width) in enumerate(parts):
            name = "qk"[n] if t == D else kind[t]
            rep = width // HD
            taps = a[f"L0_conv_w_pool_{name}"].reshape(TAPS, HD)
            vec[p:p + width, TAP0 + 9 * t:TAP0 + 9 * t + TAPS] = np.tile(taps.T, (rep, 1))
            vec[p:p + width, BQKV0 + t] = a["L0_conv_b_qkv"][col:col + width]
            vec[p:p + width, LNG0 + t] = np.tile(a[f"L0_conv_g_{name}"], rep)
            vec[p:p + width, LNB0 + t] = np.tile(a[f"L0_conv_b_{name}"], rep)
            if t in (A, B, D):
                vec[p:p + width, BQKV1 + {A: 0, B: 1, D: 2}[t]] = a["L1_conv_qkv_b"][col:col + width]
    vec[:, MASK] = -(np.arange(128) // HD % 2)
    vec[:, MASK + 1] = EPS

    rel = np.zeros((64, 4, REL), np.float32)
    for k, name in enumerate(("L0_conv_rel_pos_h", "L0_conv_rel_pos_w", "L1_conv_rel_pos_h", "L1_conv_rel_pos_w")):
        rel[:, k] = np.tile(a[name][REL - 1::-1].T, (4, 1))
    lora = np.concatenate([a["L1_conv_FacTu_w"].T, a["L1_conv_FacTv_w"], a["L1_conv_q_facts_w"], a["L1_conv_v_facts_w"]], 1)
    biases = np.zeros((16, 2 * DIM), np.float32)
    biases[0, :DIM], biases[0, DIM:] = a["L0_conv_b_proj"], a["L1_conv_proj_b"]
    lora = np.concatenate([lora, biases], 1)
    w_proj = np.zeros((HG, 4, 32, 2, DIM), np.float32)
    w_t = a["L0_conv_w_proj"].T
    w_proj[:, :, :HD, 0] = w_t.reshape(HG, 4, HD, DIM)
    w_proj[:, :, :HD, 1] = a["L1_conv_proj_w"].reshape(HG, 4, HD, DIM)
    w_proj = w_proj.reshape(HG, 128, 2, DIM).transpose(1, 2, 0, 3)
    w_proj_q = np.zeros((128, 2, DIM), np.float32)
    w_proj_q[:, 0] = w_t[:128]
    w_proj_q[:64, 1] = w_t[128:]
    arrays = {
        "x_t": a["x"].reshape(TOK, DIM).T, "w_qkv0": a["L0_conv_w_qkv"].T, "w_qkv1": a["L1_conv_qkv_w"],
        "consts": cst, "hots": hots, "vectors": vec, "neg_hot": hot, "rel": rel, "lora": lora,
        "v_bias1": np.broadcast_to(a["L1_conv_qkv_b"][2 * DIM:], (128, DIM)),
        "w_proj": w_proj, "w_proj_q": w_proj_q,
    }
    arrays = {k: np.ascontiguousarray(v) for k, v in arrays.items()}
    nc = bacc.Bacc("TRN2", target_bir_lowering=False, num_devices=1)
    args = [nc.dram_tensor(k, v.shape, F32, kind="ExternalInput").ap() for k, v in arrays.items()]
    out = nc.dram_tensor("out_t", (DIM, TOK), F32, kind="ExternalOutput").ap()
    attention_blocks(nc, *args, out)
    r = run_bass_kernel_spmd(nc, [arrays], core_ids=[0])
    y = r.results[0]["out_t"]
    return np.ascontiguousarray(y.T).reshape(1, SIDE, SIDE, DIM)
```
